# Optimizing a Trainium2 kernel written in Bass

```python
import numpy as np
import jax
import jax.numpy as jnp

def _softmax(x, axis=-1):
    return jax.nn.softmax(x, axis=axis)

def _gelu(x):
    return jax.nn.gelu(x, approximate=True)

def _silu(x):
    return jax.nn.silu(x)

def _sigmoid(x):
    return jax.nn.sigmoid(x)

def _layernorm(x, axis=-1, eps=1e-05):
    m = jnp.mean(x, axis=axis, keepdims=True)
    v = jnp.var(x, axis=axis, keepdims=True)
    return (x - m) / jnp.sqrt(v + eps)

def _scatter_add(tgt, idx, src, axis=0):
    return tgt.at[idx].add(src)

def _segment_sum(src, seg, n):
    return jax.ops.segment_sum(src, seg, n)
kernel_name = 'mk_gnn_resnorm_d1_gnn_r8_3ff2d0'

def setup_inputs(seed: int=0):
    np.random.seed(seed)
    _w = jnp.asarray

    def _rec_inputs():
        import jax
        import jax.numpy as jnp
        _gk = jax.random.key(seed)
        x = -0.0003713 + 1 * jax.random.normal(jax.random.fold_in(_gk, 1), (6250, 128), jnp.float32)
        _s = jax.random.randint(jax.random.fold_in(_gk, 2), (50000,), 0, 6250, jnp.int32)
        _d = jax.random.randint(jax.random.fold_in(_gk, 3), (50000,), 0, 6250, jnp.int32)
        _loop = jnp.arange(6250, dtype=jnp.int32)
        src = jnp.concatenate([_s, _d, _loop])
        dst = jnp.concatenate([_d, _s, _loop])
        _o = jnp.argsort(dst, stable=True)
        src = src[_o]
        dst = dst[_o]
        edge_attr_5 = 0.000254407 + 0.99978 * jax.random.normal(jax.random.fold_in(_gk, 11), (106250, 5), jnp.float32)
        return (x, src, dst, edge_attr_5)
    x, src, dst, edge_attr_5 = _rec_inputs()

    def _L0_gnn_setup():
        import jax, jax.numpy as jnp
        import numpy as np
        N_NODES = 12500
        N_EDGES = 200000
        D_IN = 128
        D_MSG = 128
        D_HID = 128
        D_EDGE = 5
        D_CAT = D_IN + D_MSG
        D_U1, D_U2, D_OUT = (214, 172, 128)

        def _leaky(x):
            return jax.nn.leaky_relu(x, negative_slope=0.01)
        key = jax.random.key(seed)
        ks = jax.random.split(key, 12)

        def kaiming(k, shape):
            fan_in = shape[1]
            gain = np.sqrt(2.0 / (1.0 + 0.01 ** 2))
            return jax.random.normal(k, shape, dtype=jnp.float32) * (gain / np.sqrt(fan_in))
        x = jax.random.normal(ks[0], (N_NODES, D_IN), dtype=jnp.float32)
        edge_index = jax.random.randint(ks[1], (2, N_EDGES), 0, N_NODES, dtype=jnp.int64)
        edge_attr = jax.random.normal(ks[2], (N_EDGES, D_EDGE), dtype=jnp.float32)
        return {'x': x, 'edge_index': edge_index, 'edge_attr': edge_attr, 'Wm1': kaiming(ks[3], (D_HID, D_EDGE)), 'bm1': jnp.zeros((D_HID,), jnp.float32), 'Wm2': kaiming(ks[4], (D_HID, D_HID)), 'bm2': jnp.zeros((D_HID,), jnp.float32), 'Wm3': kaiming(ks[5], (D_MSG, D_HID)), 'bm3': jnp.zeros((D_MSG,), jnp.float32), 'ln_g': jnp.ones((D_CAT,), jnp.float32), 'ln_b': jnp.zeros((D_CAT,), jnp.float32), 'Wu1': kaiming(ks[6], (D_U1, D_CAT)), 'bu1': jnp.zeros((D_U1,), jnp.float32), 'Wu2': kaiming(ks[7], (D_U2, D_U1)), 'bu2': jnp.zeros((D_U2,), jnp.float32), 'Wu3': kaiming(ks[8], (D_OUT, D_U2)), 'bu3': jnp.zeros((D_OUT,), jnp.float32)}
    _L0_gnn_all = _L0_gnn_setup()
    _L0_gnn_in = {k: v for k, v in _L0_gnn_all.items() if k in ('Wm1', 'bm1', 'Wm2', 'bm2', 'Wm3', 'bm3', 'ln_g', 'ln_b', 'Wu1', 'bu1', 'Wu2', 'bu2', 'Wu3', 'bu3')}
    del _L0_gnn_all
    return {'x': x, 'src': src, 'dst': dst, 'edge_attr_5': edge_attr_5, 'L0_gnn_Wm1': _L0_gnn_in['Wm1'], 'L0_gnn_bm1': _L0_gnn_in['bm1'], 'L0_gnn_Wm2': _L0_gnn_in['Wm2'], 'L0_gnn_bm2': _L0_gnn_in['bm2'], 'L0_gnn_Wm3': _L0_gnn_in['Wm3'], 'L0_gnn_bm3': _L0_gnn_in['bm3'], 'L0_gnn_ln_g': _L0_gnn_in['ln_g'], 'L0_gnn_ln_b': _L0_gnn_in['ln_b'], 'L0_gnn_Wu1': _L0_gnn_in['Wu1'], 'L0_gnn_bu1': _L0_gnn_in['bu1'], 'L0_gnn_Wu2': _L0_gnn_in['Wu2'], 'L0_gnn_bu2': _L0_gnn_in['bu2'], 'L0_gnn_Wu3': _L0_gnn_in['Wu3'], 'L0_gnn_bu3': _L0_gnn_in['bu3']}

def reference(x, src, dst, edge_attr_5, L0_gnn_Wm1, L0_gnn_bm1, L0_gnn_Wm2, L0_gnn_bm2, L0_gnn_Wm3, L0_gnn_bm3, L0_gnn_ln_g, L0_gnn_ln_b, L0_gnn_Wu1, L0_gnn_bu1, L0_gnn_Wu2, L0_gnn_bu2, L0_gnn_Wu3, L0_gnn_bu3):
    import jax
    import jax.numpy as jnp

    def _L0_gnn_ref(x, edge_index, edge_attr, Wm1, bm1, Wm2, bm2, Wm3, bm3, ln_g, ln_b, Wu1, bu1, Wu2, bu2, Wu3, bu3):
        import jax, jax.numpy as jnp
        import numpy as np
        N_NODES = 12500
        N_EDGES = 200000
        D_IN = 128
        D_MSG = 128
        D_HID = 128
        D_EDGE = 5
        D_CAT = D_IN + D_MSG
        D_U1, D_U2, D_OUT = (214, 172, 128)

        def _leaky(x):
            return jax.nn.leaky_relu(x, negative_slope=0.01)
        h = _leaky(edge_attr @ Wm1.T + bm1)
        h = _leaky(h @ Wm2.T + bm2)
        msg = h @ Wm3.T + bm3
        dst = edge_index[1]
        aggr = jax.ops.segment_sum(msg, dst, num_segments=x.shape[0])
        cat = jnp.concatenate([x, aggr], axis=-1)
        mu = jnp.mean(cat, axis=-1, keepdims=True)
        var = jnp.mean((cat - mu) ** 2, axis=-1, keepdims=True)
        nrm = (cat - mu) * jax.lax.rsqrt(var + 1e-05) * ln_g + ln_b
        u = _leaky(nrm @ Wu1.T + bu1)
        u = _leaky(u @ Wu2.T + bu2)
        return u @ Wu3.T + bu3
    edge_index = jnp.stack([src, dst])
    x = _layernorm(x + _L0_gnn_ref(x, edge_index, edge_attr_5, L0_gnn_Wm1, L0_gnn_bm1, L0_gnn_Wm2, L0_gnn_bm2, L0_gnn_Wm3, L0_gnn_bm3, L0_gnn_ln_g, L0_gnn_ln_b, L0_gnn_Wu1, L0_gnn_bu1, L0_gnn_Wu2, L0_gnn_bu2, L0_gnn_Wu3, L0_gnn_bu3), axis=-1)
    return x

_drawn_inputs = setup_inputs


def setup_inputs(seed=0):
    import zlib

    import numpy as np

    out = dict(_drawn_inputs(seed))
    spreads = {'L0_gnn_bm1': (0.0, 0.1),
     'L0_gnn_bm2': (0.0, 0.1),
     'L0_gnn_bm3': (0.0, 0.1),
     'L0_gnn_ln_g': (1.0, 0.2),
     'L0_gnn_ln_b': (0.0, 0.1),
     'L0_gnn_bu1': (0.0, 0.1),
     'L0_gnn_bu2': (0.0, 0.1),
     'L0_gnn_bu3': (0.0, 0.1)}
    factors = {}
    for name, (base, spread) in spreads.items():
        noise = np.random.default_rng([zlib.crc32(name.encode()), seed]).standard_normal(out[name].shape)
        drawn = base * np.exp(spread * noise) if base else spread * noise
        out[name] = jnp.asarray(drawn.astype(out[name].dtype))
    for name, factor in factors.items():
        out[name] = (out[name] * factor).astype(out[name].dtype)
    return out
```

```python
import concourse.bass as bass
from concourse import mybir
from contextlib import ExitStack
import numpy as np

F32 = mybir.dt.float32
BF16 = mybir.dt.bfloat16
I32 = mybir.dt.int32
ALU = mybir.AluOpType
ACT = mybir.ActivationFunctionType
AX = mybir.AxisListType

NODES, EDGES, D, DE = 6250, 106250, 128, 5
U1, U2 = 214, 172
P = 128
GT = 4
GE = GT * P
PIECE = 8192
PIECES = -(-EDGES // PIECE)
EPAD = PIECES * PIECE
GROUPS = EPAD // GE
TILES = EPAD // P
R = DE + 1
K54 = 9 * R
PC = R * PIECE // P
CHUNK = 2048
CG = CHUNK // GE
BODY = 2 * CG
TURNS = GROUPS // BODY
W = D + 1
WIN = 64
NT = -(-NODES // P)
LASTROWS = NODES - (NT - 1) * P
ST = 4
SUPERS = -(-NT // ST)
H1, H2 = U1 // 2, U2 // 2
NB = 7
SLOPE = 0.01
EPS = 1e-5


def gnn_kernel(nc, ea, dst_t, dst_g, x, wm1, wm1t, bm1, wm2t, bm2, wm3t, bm3, ln_g, ln_b,
               wu1t, bu1, wu2t, bu2, wu3t, bu3, out):
    ctx = ExitStack()
    with ctx:
        def sb(name, shape, dt=F32):
            return ctx.enter_context(nc.sbuf_tensor(name, shape, dt))

        def sem(name):
            return ctx.enter_context(nc.semaphore(name))

        parts_dram = nc.dram_tensor("parts_dram", [PIECES, K54, PIECE], BF16)
        meta_dram = nc.dram_tensor("meta_dram", [3, GROUPS], I32)

        ps = ctx.enter_context(nc.psum_tensor("ps", [P, 8, 512], F32))

        ident = sb("ident", [P, P])
        iota = sb("iota", [P, P])
        w1n = sb("w1n", [P, R])
        w1t = sb("w1t", [R, D])
        b2row = sb("b2row", [R, D])
        lin = sb("lin", [R, D])
        wres = sb("wres", [R, 2, D])
        wpart = sb("wpart", [R, 3, 2, D], BF16)
        w54 = sb("w54", [K54, 2, D], BF16)
        w2t = sb("w2t", [D, D])
        w3t = sb("w3t", [D, D])
        bm3b = sb("bm3b", [P, D])
        lng = sb("lng", [P, 2])
        lnb = sb("lnb", [P, 2])
        wu1 = sb("wu1", [P, 2, U1])
        wu2 = sb("wu2", [H1, 2, U2])
        wu3 = sb("wu3", [H2, 2, D])
        bu1c = sb("bu1c", [H1, 2])
        bu2c = sb("bu2c", [H2, 2])
        bu3b = sb("bu3b", [P, D])
        half = sb("half", [P, ST])
        eps = sb("eps", [P, ST])
        minus = sb("minus", [P, ST])

        EA_COLS, EDGE_COLS = PIECES * PC * 5 // 2, 6 * GE + 2 * GT * W + CHUNK
        shared = sb("shared", [P, EA_COLS + EDGE_COLS])
        ea_sb = shared[:, 0:PIECES * PC].rearrange("p (q c) -> p q c", c=PC)
        ea_part = shared[:, PIECES * PC:EA_COLS].bitcast(BF16).rearrange("p (k q c) -> p k q c", k=3, c=PC)

        gdst = sb("gdst", [GROUPS // 2, 2, GE], I32)
        gmin = sb("gmin", [GROUPS // 2, 2], I32)
        gmax = sb("gmax", [GROUPS // 2, 2], I32)
        gpar = sb("gpar", [GROUPS // 2, 2], I32)
        ghalf = sb("ghalf", [GROUPS // 2, 2], I32)
        gmeta = sb("gmeta", [GROUPS // 2, 3, 2], I32)
        base_b = sb("base_b", [P, GROUPS], I32)
        slot_row = sb("slot_row", [1, GROUPS], I32)
        span_row = sb("span_row", [1, GROUPS], I32)
        span_max = sb("span_max", [1, 1], I32)
        flag = sb("flag", [1, 1], I32)
        dst_sb = sb("dst_sb", [P, TILES], I32)
        dst_rel = sb("dst_rel", [P, TILES])

        taken = [EA_COLS]

        def part_of_shared(parts, *shape):
            size = int(np.prod(shape))
            view = shared[0:parts, taken[0]:taken[0] + size]
            taken[0] += size
            if len(shape) == 2:
                return view.rearrange("p (a b) -> p a b", a=shape[0])
            if len(shape) == 3:
                return view.rearrange("p (a b c) -> p a b c", a=shape[0], b=shape[1])
            return view

        a54 = part_of_shared(K54, CHUNK).bitcast(BF16).rearrange("p (b e) -> p b e", b=2)
        h1 = part_of_shared(P, 2, GE)
        relu2 = part_of_shared(P, 2, GE)
        onehot = part_of_shared(P, 2, GE)
        h2 = part_of_shared(P, 2, GT, W)
        acc = sb("acc", [P, 2, NT, W])

        shift = sb("shift", [P, NT, W])
        x_sb = sb("x_sb", [P, NT, D])
        taken[0] = 0
        xb = part_of_shared(P, NT, D)
        agg = part_of_shared(P, 2, ST, W)
        aggT = part_of_shared(P, ST * P)
        msg = part_of_shared(P, 2, ST, D)
        bn = sb("bn", [P, ST, 12])
        mv = sb("mv", [P, 2, ST, 2])
        rstd = sb("rstd", [P, 2, ST])
        mrs = sb("mrs", [P, 2, ST])
        nrm = part_of_shared(P, 2, ST, 2 * D)
        nrmT = part_of_shared(P, 2, ST * P)
        z1 = part_of_shared(H1, 2, ST * P)
        u1 = part_of_shared(H1, 2, ST * P)
        z2 = part_of_shared(H2, 2, ST * P)
        u2 = part_of_shared(H2, 2, ST * P)
        y = part_of_shared(P, 2, ST, D)
        ybn = sb("ybn", [P, ST, 6])
        ymv = sb("ymv", [P, 2, ST, 2])
        yrstd = sb("yrstd", [P, 2, ST])
        ymrs = sb("ymrs", [P, 2, ST])
        o_sb = part_of_shared(P, 2, ST, D)
        node_iota = shift[:, :, :].rearrange("p a b -> p (a b)")[:, 0:NT * P]

        weights_in = sem("weights_in")
        late_in = sem("late_in")
        b2row_zero = sem("b2row_zero")
        b2row_in = sem("b2row_in")
        x_zero = sem("x_zero")
        ea_in = [sem(f"ea_in{n}") for n in range(3)]
        dst_in = sem("dst_in")
        consts = sem("consts")
        pool_ident = sem("pool_ident")
        lin_mm = sem("lin_mm")
        wsplit = sem("wsplit")
        w54_in = sem("w54_in")
        ea_hi = sem("ea_hi")
        ea_rest = sem("ea_rest")
        ea_mid = sem("ea_mid")
        ea_lo = sem("ea_lo")
        parts_out = [sem(f"parts_out{n}") for n in range(3)]
        meta_step = sem("meta_step")
        meta_out = sem("meta_out")
        meta_in = sem("meta_in")
        rel_ready = sem("rel_ready")
        flag_ready = sem("flag_ready")
        ones_ready = sem("ones_ready")
        acc_zero = sem("acc_zero")

        chunk_in = [sem(f"chunk_in{n}") for n in range(2)]
        s1_done = sem("s1_done")
        h1_ready = sem("h1_ready")
        s2_done = sem("s2_done")
        relu2_ready = sem("relu2_ready")
        h2_ready = sem("h2_ready")
        onehot_ready = sem("onehot_ready")
        s3_done = sem("s3_done")
        acc_done = sem("acc_done")

        g_tile_in = sem("g_tile_in")
        g_iota = sem("g_iota")
        g_s1_done = sem("g_s1_done")
        g_h1_ready = sem("g_h1_ready")
        g_s2_done = sem("g_s2_done")
        g_relu2_ready = sem("g_relu2_ready")
        g_h2_ready = sem("g_h2_ready")
        g_onehot = sem("g_onehot")
        g_s3_done = sem("g_s3_done")
        g_acc_done = sem("g_acc_done")

        edges_done = sem("edges_done")
        shift_in = [sem(f"shift_in{n}") for n in range(2)]
        agg_ready = sem("agg_ready")
        a1_done = sem("a1_done")
        aggT_ready = sem("aggT_ready")
        a2_done = sem("a2_done")
        msg_ready = sem("msg_ready")
        bn_ready = sem("bn_ready")
        stats_ready = sem("stats_ready")
        rstd_step = sem("rstd_step")
        nrm_ready = sem("nrm_ready")
        xb_ready = sem("xb_ready")
        t_done = sem("t_done")
        nrmT_ready = sem("nrmT_ready")
        u1_done = sem("u1_done")
        z1_ready = sem("z1_ready")
        u1_ready = sem("u1_ready")
        u2_done = sem("u2_done")
        z2_ready = sem("z2_ready")
        u2_ready = sem("u2_ready")
        u3_done = sem("u3_done")
        y_ready = sem("y_ready")
        ybn_ready = sem("ybn_ready")
        ystats_ready = sem("ystats_ready")
        yrstd_step = sem("yrstd_step")
        rstd_ready = sem("rstd_ready")
        yrstd_ready = sem("yrstd_ready")
        out_ready = sem("out_ready")
        out_stored = [sem(f"out_stored{n}") for n in range(2)]

        BATCHES = [(0, 1), (1, 5), (5, PIECES)]
        N_WEIGHTS, N_LATE = 4, 14

        def node_steps(eng, step, first, last):
            lo, hi = 3, 9
            for s in range(first, lo):
                step(s, s % 2, lambda q, s=s: 0 <= s + q < SUPERS, s)
            with eng.Fori(0, (hi - lo) // 2) as i:
                for j in range(2):
                    step(2 * i + lo + j, (lo + j) % 2, lambda q: True, None)
            for s in range(hi, last + 1):
                step(s, s % 2, lambda q, s=s: 0 <= s + q < SUPERS, s)

        def tiles_of(s, q, static):
            return ST if static is None or static + q < SUPERS - 1 else NT - ST * (SUPERS - 1)

        def from_tile(s, q):
            return (s + q) * ST

        assert taken[0] <= EA_COLS + EDGE_COLS
        block = ctx.enter_context(nc.Block())

        @block.sync
        def _(sp):
            sp.dma_start(ea_sb[:, 0, :], ea[0]).then_inc(ea_in[0], 16)
            sp.dma_start(gdst[:, :, :], dst_g.rearrange("p (a e) -> p a e", a=2)).then_inc(dst_in, 16)
            sp.dma_start(dst_sb[:, :], dst_t).then_inc(dst_in, 16)
            for n in (1, 2):
                a, b = BATCHES[n]
                sp.dma_start(ea_sb[:, a:b, :], ea[a:b].rearrange("q p c -> p q c")).then_inc(ea_in[n], 16)
            sp.wait_ge(meta_step, 6)
            for kind in range(3):
                sp.dma_start(meta_dram[kind, :].rearrange("(p a) -> p a", a=2), gmeta[:, kind, :]).then_inc(meta_out, 16)
            sp.wait_ge(meta_out, 48)
            sp.dma_start(base_b[:, :], meta_dram[0, :].partition_broadcast(P)).then_inc(meta_in, 16)
            sp.dma_start(slot_row[:, :], meta_dram[1:2, :]).then_inc(meta_in, 16)
            sp.dma_start(span_row[:, :], meta_dram[2:3, :]).then_inc(meta_in, 16)

            sp.wait_ge(parts_out[0], 16 * 9)
            sp.wait_ge(flag_ready, 1)
            general = sp.value_load(flag[0:1, 0:1], min_val=0, max_val=1)
            with sp.If(general < 1):
                def load_chunk(piece, k, c):
                    if not isinstance(c, int) or c >= 2:
                        sp.wait_ge(s2_done, CG * (c - 1))
                    sp.dma_start(a54[:, k % 2, :], parts_dram[piece, :, k * CHUNK:(k + 1) * CHUNK])\
                        .then_inc(chunk_in[k % 2], 16)

                for piece in range(2):
                    for k in range(PIECE // CHUNK):
                        if (piece, k) == (1, 0):
                            sp.wait_ge(parts_out[1], 16 * 9)
                        load_chunk(piece, k, piece * (PIECE // CHUNK) + k)
                sp.wait_ge(parts_out[2], 16 * 9)
                with sp.Fori(2, PIECES) as piece:
                    for k in range(PIECE // CHUNK):
                        load_chunk(piece, k, piece * (PIECE // CHUNK) + k)
            with sp.Else():
                sp.wait_ge(parts_out[1], 16 * 9)
                sp.wait_ge(parts_out[2], 16 * 9)
                with sp.Fori(0, PIECES) as piece:
                    with sp.Fori(0, PIECE // P) as k:
                        sp.wait_ge(g_s2_done, piece * (PIECE // P) + k + 1)
                        sp.dma_start(a54[:, 0, 0:P], parts_dram[bass.ds(piece, 1), :, bass.ds(k * P, P)]
                                     .rearrange("q r n -> (q r) n")).then_inc(g_tile_in, 16)

            sp.wait_ge(edges_done, 1)
            for n, (a, b) in enumerate([(0, 2 * ST), (2 * ST, NT)]):
                lo = max(a, 1)
                sp.dma_start(shift[0:WIN, lo:b, :], acc[WIN:P, 1, lo - 1:b - 1, :]).then_inc(shift_in[n], 16)
                sp.dma_start(shift[WIN:P, a:b, :], acc[0:WIN, 1, a:b, :]).then_inc(shift_in[n], 16)

            for s in range(SUPERS):
                t0 = s * ST * P
                sp.wait_ge(out_ready, s + 1)
                if s < SUPERS - 1:
                    sp.dma_start(out[t0:t0 + ST * P, :].rearrange("(t p) f -> p t f", p=P), o_sb[:, s % 2, :, :])\
                        .then_inc(out_stored[s % 2], 16)
                else:
                    sp.dma_start(out[t0:NODES, :], o_sb[0:LASTROWS, s % 2, 0, :]).then_inc(out_stored[s % 2], 16)
            sp.wait_ge(out_stored[0], 16 * ((SUPERS + 1) // 2))
            sp.wait_ge(out_stored[1], 16 * (SUPERS // 2))

        @block.scalar
        def _(act):
            act.dma_start(w1n[:, 0:DE], wm1).then_inc(weights_in, 16)
            act.dma_start(w1n[:, DE:R], bm1.rearrange("(p a) -> p a", a=1)).then_inc(weights_in, 16)
            act.dma_start(w1t[0:DE, :], wm1t).then_inc(weights_in, 16)
            act.dma_start(w1t[DE:R, :], bm1.rearrange("(a p) -> a p", a=1)).then_inc(weights_in, 16)
            act.dma_start(w2t[:, :], wm2t).then_inc(weights_in, 16)
            act.wait_ge(b2row_zero, 1)
            act.dma_start(b2row[DE:R, :], bm2.rearrange("(a p) -> a p", a=1)).then_inc(b2row_in, 16)

            def stacked_out(n):
                a, b = BATCHES[n]
                for p in range(3):
                    for rep in range(3):
                        row = (p * 3 + rep) * R
                        act.dma_start(
                            parts_dram[a:b, row:row + R, :].rearrange("q r n -> q (r n)")
                            .rearrange("q (x c) -> x q c", x=P),
                            ea_part[:, p, a:b, :]).then_inc(parts_out[n], 16)

            for n, (a, b) in enumerate(BATCHES):
                act.wait_ge(ea_in[n], 16)
                act.activation(ea_part[:, 0, a:b, :], ea_sb[:, a:b, :], ACT.Copy).then_inc(ea_hi, 1)
                act.wait_ge(ea_rest, n + 1)
                act.activation(ea_part[:, 1, a:b, :], ea_sb[:, a:b, :], ACT.Copy).then_inc(ea_mid, 1)
                if n == 0:
                    act.wait_ge(wsplit, 3)
                    for p in range(3):
                        for rep in range(3):
                            row = (p * 3 + rep) * R
                            act.dma_start(w54[row:row + R, :, :], wpart[:, rep, :, :]).then_inc(w54_in, 16)
                act.wait_ge(ea_lo, n + 1)
                stacked_out(n)

            act.dma_start(w3t[:, :], wm3t).then_inc(late_in, 16)
            act.dma_start(bm3b[:, :], bm3.partition_broadcast(P)).then_inc(late_in, 16)
            act.dma_start(lng[:, :], ln_g.rearrange("(a p) -> p a", p=P), allow_slow_non_contiguous=True).then_inc(late_in, 16)
            act.dma_start(lnb[:, :], ln_b.rearrange("(a p) -> p a", p=P), allow_slow_non_contiguous=True).then_inc(late_in, 16)
            act.dma_start(wu1[:, :, :], wu1t.rearrange("(a p) m -> p a m", p=P)).then_inc(late_in, 16)
            act.dma_start(wu2[:, :, :], wu2t.rearrange("(a p) m -> p a m", p=H1)).then_inc(late_in, 16)
            act.dma_start(wu3[:, :, :], wu3t.rearrange("(a p) m -> p a m", p=H2)).then_inc(late_in, 16)
            act.dma_start(bu1c[:, :], bu1.rearrange("(a p) -> p a", p=H1), allow_slow_non_contiguous=True).then_inc(late_in, 16)
            act.dma_start(bu2c[:, :], bu2.rearrange("(a p) -> p a", p=H2), allow_slow_non_contiguous=True).then_inc(late_in, 16)
            act.dma_start(bu3b[:, :], bu3.partition_broadcast(P)).then_inc(late_in, 16)
            xt = (NT - 1) * P
            for q in range(3):
                a, b = q * 16, (q + 1) * 16
                act.dma_start(x_sb[:, a:b, :], x[a * P:b * P, :].rearrange("(t p) f -> p t f", p=P)).then_inc(late_in, 16)
            act.wait_ge(x_zero, 1)
            act.dma_start(x_sb[0:LASTROWS, NT - 1, :], x[xt:NODES, :]).then_inc(late_in, 16)

            act.wait_ge(flag_ready, 1)
            general = act.value_load(flag[0:1, 0:1], min_val=0, max_val=1)
            with act.If(general < 1):
                def first_relu(g, j, peeled):
                    act.wait_ge(s1_done, g + 1)
                    if not (peeled and g < 2):
                        act.wait_ge(s2_done, g - 1)
                    act.activation(h1[:, j % 2, :], ps[:, j % 2, :], ACT.Relu, scale=1.0 - SLOPE).then_inc(h1_ready, 1)

                def second_relu(g, j, peeled):
                    act.wait_ge(s2_done, g + 1)
                    if not (peeled and g < 2):
                        act.wait_ge(h2_ready, g - 1)
                    act.activation(relu2[:, j % 2, :], ps[:, 2 + j % 2, :], ACT.Relu, scale=1.0 - SLOPE)\
                        .then_inc(relu2_ready, 1)

                def act_edge_step(s, j, peeled):
                    first_relu(s, j, peeled)
                    if not (peeled and s < 1):
                        second_relu(s - 1, (j - 1) % BODY, peeled)

                for j in range(BODY):
                    act_edge_step(j, j, True)
                with act.Fori(1, TURNS) as i:
                    for j in range(BODY):
                        act_edge_step(i * BODY + j, j, False)
                second_relu(GROUPS - 1, BODY - 1, True)
            with act.Else():
                with act.Fori(0, TILES) as t:
                    act.wait_ge(g_s1_done, t + 1)
                    act.activation(h1[:, 0, 0:P], ps[:, 0, 0:P], ACT.Relu, scale=1.0 - SLOPE).then_inc(g_h1_ready, 1)
                    act.wait_ge(g_s2_done, t + 2)
                    act.activation(relu2[:, 0, 0:P], ps[:, 1, 0:P], ACT.Relu, scale=1.0 - SLOPE).then_inc(g_relu2_ready, 1)

            act.wait_ge(late_in, 16 * N_LATE)

            def copy_aggT(s, q, static):
                nt = tiles_of(s, q, static)
                act.wait_ge(a1_done, s + q + 1)
                if static is None or static + q >= 1:
                    act.wait_ge(a2_done, s + q)
                act.activation(aggT[:, 0:nt * P], ps[:, 0, 0:nt * P], ACT.Copy).then_inc(aggT_ready, 1)

            def scale_nrmT(s, static):
                n = tiles_of(s, 0, static) * P
                act.wait_ge(t_done, s + 1)
                if static is None or static >= 1:
                    act.wait_ge(u1_done, s)
                for h in range(2):
                    last = act.activation(nrmT[:, h, 0:n], ps[:, 1 + h, 0:n], ACT.Identity,
                                          bias=lnb[:, h:h + 1], scale=lng[:, h:h + 1])
                last.then_inc(nrmT_ready, 1)

            def add_bias(s, static, done, read, z, bank, bias, rows, ready):
                n = tiles_of(s, 0, static) * P
                act.wait_ge(done, s + 1)
                if static is None or static >= 1:
                    act.wait_ge(read, s)
                for h in range(2):
                    last = act.activation(z[:, h, 0:n], ps[0:rows, bank + h, 0:n], ACT.Identity, bias=bias[:, h:h + 1])
                last.then_inc(ready, 1)

            def normalise(s, q, par, static):
                nt = tiles_of(s, q, static)
                t0 = from_tile(s, q)
                b = par
                act.wait_ge(rstd_ready, s + q + 1)
                if static is None or static + q >= 2:
                    act.wait_ge(t_done, s + q - 1)
                for t in range(nt):
                    act.activation(nrm[:, b, t, 0:D], x_sb[:, bass.ds(t0 + t, 1), :].rearrange("p a f -> p (a f)"),
                                   ACT.Identity, bias=mrs[:, b, t:t + 1], scale=rstd[:, b, t:t + 1])
                    last = act.activation(nrm[:, b, t, D:2 * D], msg[:, b, t, :], ACT.Identity,
                                          bias=mrs[:, b, t:t + 1], scale=rstd[:, b, t:t + 1])
                last.then_inc(nrm_ready, 1)

            def finish(s, q, par, static):
                nt = tiles_of(s, q, static)
                b = 1 - par
                act.wait_ge(yrstd_ready, s + q + 1)
                if static is None:
                    act.wait_ge(out_stored[b], (s + q - b) * 8)
                elif static + q >= 2:
                    act.wait_ge(out_stored[b], 16 * ((static + q - b) // 2))
                for t in range(nt):
                    last = act.activation(o_sb[:, b, t, :], y[:, b, t, :], ACT.Identity,
                                          bias=ymrs[:, b, t:t + 1], scale=yrstd[:, b, t:t + 1])
                last.then_inc(out_ready, 1)

            def act_step(s, par, has, static):
                if has(0):
                    scale_nrmT(s, static)
                if has(2):
                    copy_aggT(s, 2, static)
                if has(0):
                    add_bias(s, static, u1_done, u1_ready, z1, 3, bu1c, H1, z1_ready)
                if has(-1):
                    finish(s, -1, par, static)
                if has(0):
                    add_bias(s, static, u2_done, u2_ready, z2, 5, bu2c, H2, z2_ready)
                if has(2):
                    normalise(s, 2, par, static)

            node_steps(act, act_step, -2, SUPERS)

        @block.gpsimd
        def _(pool):
            pool.memset(b2row[:, :], 0.0).then_inc(b2row_zero, 1)
            pool.iota(iota[:, :], pattern=[[1, P]], base=0, channel_multiplier=0,
                      allow_small_or_imprecise_dtypes=True).then_inc(consts, 1)
            pool.memset(h2[:, :, :, D:W], 1.0).then_inc(ones_ready, 1)
            pool.memset(acc[:, :, :, :], 0.0).then_inc(acc_zero, 1)
            pool.memset(x_sb[:, NT - 1, :], 0.0).then_inc(x_zero, 1)
            pool.memset(half[:, :], -0.5).then_inc(consts, 1)
            pool.memset(eps[:, :], EPS).then_inc(consts, 1)
            pool.memset(minus[:, :], -1.0).then_inc(consts, 1)
            pool.memset(ident[:, :], 0.0).then_inc(pool_ident, 1)
            pool.wait_ge(pool_ident, 1)
            pool.affine_select(out=ident[:, :], in_=ident[:, :], compare_op=ALU.not_equal, fill=1.0,
                               base=0, pattern=[[-1, P]], channel_multiplier=1).then_inc(pool_ident, 1)

            pool.wait_ge(late_in, 16 * N_LATE)
            for n in range(3):
                pool.wait_ge(parts_out[n], 16 * 9)
            pool.tensor_tensor(xb[:, :, :], x_sb[:, :, :], bu3b[:, :].unsqueeze(1).to_broadcast([P, NT, D]), ALU.add)\
                .then_inc(xb_ready, 1)

            pool.wait_ge(flag_ready, 1)
            general = pool.value_load(flag[0:1, 0:1], min_val=0, max_val=1)
            with pool.If(general > 0):
                pool.iota(node_iota, pattern=[[1, NT * P]], base=0, channel_multiplier=0,
                          allow_small_or_imprecise_dtypes=True).then_inc(g_iota, 1)

            pool.wait_ge(consts, 4)

            def scales(n, nt, b, ready, step, used, used_from, mv_, r, m, done):
                pool.wait_ge(ready, n + 1)
                if used_from:
                    pool.wait_ge(used, n - 1)
                pool.tensor_tensor(r[:, b, 0:nt], mv_[:, b, 0:nt, 1], eps[:, 0:nt], ALU.add).then_inc(step, 1)
                pool.wait_ge(step, 3 * n + 1)
                pool.tensor_tensor(r[:, b, 0:nt], r[:, b, 0:nt], half[:, 0:nt], ALU.pow).then_inc(step, 1)
                pool.wait_ge(step, 3 * n + 2)
                pool.tensor_tensor(m[:, b, 0:nt], mv_[:, b, 0:nt, 0], r[:, b, 0:nt], ALU.mult).then_inc(step, 1)
                pool.wait_ge(step, 3 * n + 3)
                pool.tensor_tensor(m[:, b, 0:nt], m[:, b, 0:nt], minus[:, 0:nt], ALU.mult).then_inc(done, 1)

            def pool_step(s, par, has, static):
                if has(-1):
                    scales(s - 1, tiles_of(s, -1, static), 1 - par, ystats_ready, yrstd_step, out_ready,
                           static is None or static >= 3, ymv, yrstd, ymrs, yrstd_ready)
                if has(2):
                    scales(s + 2, tiles_of(s, 2, static), par, stats_ready, rstd_step, nrm_ready,
                           static is None or static >= 0, mv, rstd, mrs, rstd_ready)

            node_steps(pool, pool_step, -2, SUPERS)

        @block.vector
        def _(dve):
            dve.wait_ge(dst_in, 32)
            dve.tensor_reduce(gmin[:, :], gdst[:, :, :], AX.X, ALU.min).then_inc(meta_step, 1)
            dve.tensor_reduce(gmax[:, :], gdst[:, :, :], AX.X, ALU.max).then_inc(meta_step, 1)
            dve.wait_ge(meta_step, 2)
            dve.tensor_scalar(gmeta[:, 0, :], gmin[:, :], -WIN, None, ALU.bitwise_and).then_inc(meta_step, 1)
            dve.tensor_scalar(gpar[:, :], gmin[:, :], 6, 1, ALU.logical_shift_right, ALU.bitwise_and)
            dve.tensor_scalar(ghalf[:, :], gmin[:, :], 7, None, ALU.logical_shift_right).then_inc(meta_step, 1)
            dve.wait_ge(meta_step, 4)
            dve.tensor_tensor(gmeta[:, 2, :], gmax[:, :], gmeta[:, 0, :], ALU.subtract).then_inc(meta_step, 1)
            dve.scalar_tensor_tensor(out=gmeta[:, 1, :], in0=gpar[:, :], scalar=float(NT), in1=ghalf[:, :],
                                     op0=ALU.mult, op1=ALU.add).then_inc(meta_step, 1)

            dve.wait_ge(lin_mm, 1)
            dve.wait_ge(b2row_in, 16)
            dve.scalar_tensor_tensor(out=wres[:, 1, :], in0=ps[0:R, 7, 0:D], scalar=SLOPE, in1=b2row[:, :],
                                     op0=ALU.mult, op1=ALU.add)
            dve.tensor_copy(wres[:, 0, :], w1t[:, :]).then_inc(wsplit, 1)
            dve.wait_ge(wsplit, 1)
            for part in range(3):
                dve.tensor_copy(wpart[:, part, :, :], wres[:, :, :]).then_inc(wsplit, 1)
                if part < 2:
                    dve.wait_ge(wsplit, 2 + 2 * part)
                    dve.tensor_tensor(wres[:, :, :], wres[:, :, :], wpart[:, part, :, :], ALU.subtract).then_inc(wsplit, 1)
                    dve.wait_ge(wsplit, 3 + 2 * part)

            for n, (a, b) in enumerate(BATCHES):
                dve.wait_ge(ea_hi, n + 1)
                dve.tensor_tensor(ea_sb[:, a:b, :], ea_sb[:, a:b, :], ea_part[:, 0, a:b, :], ALU.subtract).then_inc(ea_rest, 1)
                dve.wait_ge(ea_mid, n + 1)
                dve.tensor_tensor(ea_part[:, 2, a:b, :], ea_sb[:, a:b, :], ea_part[:, 1, a:b, :], ALU.subtract).then_inc(ea_lo, 1)
                if n == 0:
                    dve.wait_ge(meta_in, 48)
                    dve.tensor_tensor(dst_rel[:, :].rearrange("p (g t) -> p g t", t=GT),
                                      dst_sb[:, :].rearrange("p (g t) -> p g t", t=GT),
                                      base_b[:, :].unsqueeze(2).to_broadcast([P, GROUPS, GT]),
                                      ALU.subtract).then_inc(rel_ready, 1)
                    dve.tensor_reduce(span_max[:, :], span_row[:, :], AX.X, ALU.max).then_inc(meta_step, 1)
                    dve.wait_ge(meta_step, 7)
                    dve.tensor_scalar(flag[:, :], span_max[:, :], float(P), None, ALU.is_ge).then_inc(flag_ready, 1)

            dve.wait_ge(ones_ready, 1)
            dve.wait_ge(acc_zero, 1)
            dve.wait_ge(consts, 1)
            dve.wait_ge(flag_ready, 1)
            general = dve.value_load(flag[0:1, 0:1], min_val=0, max_val=1)

            def leaky(out_, in_):
                return dve.scalar_tensor_tensor(out=out_, in0=in_, scalar=SLOPE, in1=in_, op0=ALU.mult, op1=ALU.max)

            def leaky_sum(out_, z, relu):
                return dve.scalar_tensor_tensor(out=out_, in0=z, scalar=SLOPE, in1=relu, op0=ALU.mult, op1=ALU.add)

            with dve.If(general < 1):
                def second_leaky(g, j, peeled):
                    dve.wait_ge(relu2_ready, g + 1)
                    if not (peeled and g < 2):
                        dve.wait_ge(s3_done, g - 1)
                    leaky_sum(h2[:, j % 2, :, 0:D], ps[:, 2 + j % 2, :].rearrange("p (t f) -> p t f", t=GT),
                              relu2[:, j % 2, :].rearrange("p (t f) -> p t f", t=GT))\
                        .then_inc(h2_ready, 1)

                def make_onehot(g, j, peeled):
                    if not (peeled and g < 2):
                        dve.wait_ge(s3_done, g - 1)
                    dve.tensor_tensor(onehot[:, j % 2, :].rearrange("p (t n) -> p t n", n=P),
                                      iota[:, :].unsqueeze(1).to_broadcast([P, GT, P]),
                                      dst_rel[:, bass.ds(g * GT, GT)].unsqueeze(2).to_broadcast([P, GT, P]),
                                      ALU.is_equal).then_inc(onehot_ready, 1)

                def add_window(g, j, peeled):
                    slot = dve.value_load(slot_row[0:1, bass.ds(g, 1)], min_val=0, max_val=2 * NT - 1)
                    dst = acc[:, :, :, :].rearrange("p a b c -> p (a b) c")[:, bass.ds(slot, 1), :]\
                        .rearrange("p a c -> p (a c)")
                    dve.wait_ge(s3_done, g + 1)
                    if not (peeled and g < 1):
                        dve.wait_ge(acc_done, g)
                    dve.tensor_tensor(dst, ps[:, 4 + j % 2, 0:W], dst, ALU.add).then_inc(acc_done, 1)

                def dve_edge_step(s, j, peeled):
                    make_onehot(s, j, peeled)
                    if not (peeled and s < 1):
                        second_leaky(s - 1, (j - 1) % BODY, peeled)
                    if not (peeled and s < 2):
                        add_window(s - 2, (j - 2) % BODY, peeled)

                for j in range(BODY):
                    dve_edge_step(j, j, True)
                with dve.Fori(1, TURNS) as i:
                    for j in range(BODY):
                        dve_edge_step(i * BODY + j, j, False)
                second_leaky(GROUPS - 1, BODY - 1, True)
                add_window(GROUPS - 2, BODY - 2, True)
                add_window(GROUPS - 1, BODY - 1, True)
                dve.wait_ge(acc_done, GROUPS)
            with dve.Else():
                dve.wait_ge(g_iota, 1)
                with dve.Fori(0, TILES) as t:
                    dve.wait_ge(g_relu2_ready, t + 1)
                    leaky_sum(h2[:, 0, 0, 0:D], ps[:, 1, 0:P], relu2[:, 0, 0:P]).then_inc(g_h2_ready, 1)
                    for w in range(NB):
                        n = t * NB + w
                        dve.tensor_scalar(onehot[:, :, :].rearrange("p a b -> p (a b)")[:, 0:NB * P],
                                          node_iota[:, w * NB * P:(w + 1) * NB * P],
                                          dst_sb[:, bass.ds(t, 1)], None, ALU.is_equal).then_inc(g_onehot, 1)
                        dve.wait_ge(g_s3_done, n + 1)
                        for bank, (a, b) in enumerate([(0, 3), (3, 6), (6, NB)]):
                            dst = acc[:, 0, w * NB + a:w * NB + b, :]
                            last = dve.tensor_tensor(
                                dst, ps[:, 2 + bank, 0:(b - a) * W].rearrange("p (a c) -> p a c", c=W), dst, ALU.add)
                        last.then_inc(g_acc_done, 1)
                        dve.wait_ge(g_acc_done, n + 1)
            dve.memset(shift[0:WIN, 0, :], 0.0).then_inc(edges_done, 1)
            dve.wait_ge(late_in, 16 * N_LATE)
            dve.wait_ge(xb_ready, 1)
            dve.wait_ge(shift_in[0], 32)
            dve.wait_ge(edges_done, 1)

            def gather(s, q, par, static):
                nt = tiles_of(s, q, static)
                t0 = from_tile(s, q)
                b = 1 - par
                if static is not None and static + q == 2:
                    dve.wait_ge(shift_in[1], 32)
                if static is None or static + q >= 2:
                    dve.wait_ge(a1_done, s + q - 1)
                dve.tensor_tensor(agg[:, b, 0:nt, :], acc[:, 0, bass.ds(t0, nt), :], shift[:, bass.ds(t0, nt), :],
                                  ALU.add).then_inc(agg_ready, 1)

            def messages(s, q, par, static):
                nt = tiles_of(s, q, static)
                t0 = from_tile(s, q)
                b = par
                dve.wait_ge(a2_done, s + q + 1)
                dve.wait_ge(agg_ready, s + q + 1)
                if static is None or static + q >= 2:
                    dve.wait_ge(nrm_ready, s + q - 1)
                for t in range(nt):
                    last = dve.scalar_tensor_tensor(out=msg[:, b, t, :], in0=bm3b[:, :], scalar=agg[:, b, t, D:W],
                                                    in1=ps[:, 0, t * P:(t + 1) * P], op0=ALU.mult, op1=ALU.add)
                last.then_inc(msg_ready, 1)
                for t in range(nt):
                    dve.bn_stats(bn[:, t, 0:6], x_sb[:, bass.ds(t0 + t, 1), :].rearrange("p a f -> p (a f)"))
                dve.wait_ge(msg_ready, s + q + 1)
                for t in range(nt):
                    last = dve.bn_stats(bn[:, t, 6:12], msg[:, b, t, :])
                last.then_inc(bn_ready, 1)

            def moments(s, q, par, static):
                for t in range(tiles_of(s, q, static)):
                    last = dve.bn_aggr(mv[:, par, t, :], bn[:, t, :])
                last.then_inc(stats_ready, 1)

            def mlp_leaky(s, static, z_ready, read, u, z, ready):
                n = tiles_of(s, 0, static) * P
                dve.wait_ge(z_ready, s + 1)
                if static is None or static >= 1:
                    dve.wait_ge(read, s)
                leaky(u[:, :, 0:n], z[:, :, 0:n]).then_inc(ready, 1)

            def residual(s, q, par, static):
                nt = tiles_of(s, q, static)
                t0 = from_tile(s, q)
                b = 1 - par
                dve.wait_ge(u3_done, s + q + 1)
                if static is None or static + q >= 2:
                    dve.wait_ge(out_ready, s + q - 1)
                dve.tensor_tensor(y[:, b, 0:nt, :], ps[:, 7, 0:nt * P].rearrange("p (t f) -> p t f", f=D),
                                  xb[:, bass.ds(t0, nt), :], ALU.add).then_inc(y_ready, 1)
                dve.wait_ge(y_ready, s + q + 1)
                for t in range(nt):
                    last = dve.bn_stats(ybn[:, t, :], y[:, b, t, :])
                last.then_inc(ybn_ready, 1)

            def y_moments(s, q, par, static):
                for t in range(tiles_of(s, q, static)):
                    last = dve.bn_aggr(ymv[:, 1 - par, t, :], ybn[:, t, :])
                last.then_inc(ystats_ready, 1)

            def dve_step(s, par, has, static):
                if has(-1):
                    residual(s, -1, par, static)
                    dve.wait_ge(ybn_ready, s)
                if has(0):
                    mlp_leaky(s, static, z1_ready, u2_done, u1, z1, u1_ready)
                if has(-1):
                    y_moments(s, -1, par, static)
                if has(2):
                    messages(s, 2, par, static)
                    dve.wait_ge(bn_ready, s + 3)
                if has(3):
                    gather(s, 3, par, static)
                if has(2):
                    moments(s, 2, par, static)
                if has(0):
                    mlp_leaky(s, static, z2_ready, u3_done, u2, z2, u2_ready)

            node_steps(dve, dve_step, -3, SUPERS)

        @block.tensor
        def _(pe):
            pe.wait_ge(weights_in, 16 * 5)
            pe.matmul(ps[0:R, 7, 0:D], w1n[:, :], w2t[:, :], start=True, stop=True).then_inc(lin_mm, 1)
            pe.wait_ge(w54_in, 16 * 9)
            pe.wait_ge(flag_ready, 1)
            general = pe.value_load(flag[0:1, 0:1], min_val=0, max_val=1)
            with pe.If(general < 1):
                def layer1(g, j, turn, peeled):
                    if j % CG == 0:
                        pe.wait_ge(chunk_in[j // CG], 16 * (turn + 1))
                    if not (peeled and g < 2):
                        pe.wait_ge(h1_ready, g - 1)
                    e0 = (j % CG) * GE
                    pe.matmul(ps[:, j % 2, :], w54[:, 0, :], a54[:, j // CG, e0:e0 + GE],
                              start=True, stop=True).then_inc(s1_done, 1)

                def layer2(g, j, peeled):
                    pe.wait_ge(h1_ready, g + 1)
                    if not (peeled and g < 2):
                        pe.wait_ge(h2_ready, g - 1)
                    for t in range(GT):
                        e0 = (j % CG) * GE + t * P
                        cols = ps[:, 2 + j % 2, t * P:(t + 1) * P]
                        pe.matmul(cols, a54[:, j // CG, e0:e0 + P], w54[:, 1, :], start=True, stop=False)
                        last = pe.matmul(cols, h1[:, j % 2, t * P:(t + 1) * P], w2t[:, :], start=False, stop=True)
                    last.then_inc(s2_done, 1)

                def edge_sum(g, j, peeled):
                    pe.wait_ge(h2_ready, g + 1)
                    pe.wait_ge(onehot_ready, g + 1)
                    if not (peeled and g < 2):
                        pe.wait_ge(acc_done, g - 1)
                    for t in range(GT):
                        last = pe.matmul(ps[:, 4 + j % 2, 0:W], onehot[:, j % 2, t * P:(t + 1) * P],
                                         h2[:, j % 2, t, :], start=t == 0, stop=t == GT - 1)
                    last.then_inc(s3_done, 1)

                def pe_edge_step(s, j, turn, peeled):
                    layer1(s, j, turn, peeled)
                    if not (peeled and s < 1):
                        layer2(s - 1, (j - 1) % BODY, peeled)
                    if not (peeled and s < 2):
                        edge_sum(s - 2, (j - 2) % BODY, peeled)

                pe.wait_ge(ones_ready, 1)
                for j in range(BODY):
                    pe_edge_step(j, j, 0, True)
                with pe.Fori(1, TURNS) as i:
                    for j in range(BODY):
                        pe_edge_step(i * BODY + j, j, i, False)
                layer2(GROUPS - 1, BODY - 1, True)
                edge_sum(GROUPS - 2, BODY - 2, True)
                edge_sum(GROUPS - 1, BODY - 1, True)
            with pe.Else():
                pe.wait_ge(ones_ready, 1)
                pe.sem_inc(g_s2_done, 1)
                with pe.Fori(0, TILES) as t:
                    pe.wait_ge(g_tile_in, 16 * (t + 1))
                    pe.matmul(ps[:, 0, 0:P], w54[:, 0, :], a54[:, 0, 0:P], start=True, stop=True).then_inc(g_s1_done, 1)
                    pe.wait_ge(g_h1_ready, t + 1)
                    pe.matmul(ps[:, 1, 0:P], a54[:, 0, 0:P], w54[:, 1, :], start=True, stop=False)
                    pe.matmul(ps[:, 1, 0:P], h1[:, 0, 0:P], w2t[:, :], start=False, stop=True).then_inc(g_s2_done, 1)
                    pe.wait_ge(g_h2_ready, t + 1)
                    for w in range(NB):
                        pe.wait_ge(g_onehot, t * NB + w + 1)
                        for k in range(NB):
                            last = pe.matmul(ps[:, 2 + k // 3, (k % 3) * W:(k % 3 + 1) * W],
                                             onehot[:, k * P // GE, k * P % GE:k * P % GE + P],
                                             h2[:, 0, 0, :], start=True, stop=True)
                        last.then_inc(g_s3_done, 1)

            pe.wait_ge(pool_ident, 2)
            pe.wait_ge(late_in, 16 * N_LATE)

            def transpose_agg(s, q, par, static):
                nt = tiles_of(s, q, static)
                pe.wait_ge(agg_ready, s + q + 1)
                if static is None or static + q >= 1:
                    pe.wait_ge(msg_ready, s + q)
                for t in range(nt):
                    last = pe.transpose(ps[:, 0, t * P:(t + 1) * P], agg[:, par, t, 0:D], ident[:, :])
                last.then_inc(a1_done, 1)

            def product_msg(s, q, static):
                nt = tiles_of(s, q, static)
                pe.wait_ge(aggT_ready, s + q + 1)
                for t in range(nt):
                    last = pe.matmul(ps[:, 0, t * P:(t + 1) * P], aggT[:, t * P:(t + 1) * P], w3t[:, :],
                                     start=True, stop=True)
                last.then_inc(a2_done, 1)

            def transpose_nrm(s, par, static):
                nt = tiles_of(s, 0, static)
                pe.wait_ge(nrm_ready, s + 1)
                if static is None or static >= 1:
                    pe.wait_ge(nrmT_ready, s)
                for h in range(2):
                    for t in range(nt):
                        last = pe.transpose(ps[:, 1 + h, t * P:(t + 1) * P], nrm[:, par, t, h * D:(h + 1) * D], ident[:, :])
                last.then_inc(t_done, 1)

            def mlp_layer(s, static, in_ready, read, bank, w, act_in, rows, done):
                n = tiles_of(s, 0, static) * P
                pe.wait_ge(in_ready, s + 1)
                if static is None or static >= 1:
                    pe.wait_ge(read, s)
                for m in range(2):
                    for k in range(2):
                        last = pe.matmul(ps[0:rows, bank + m, 0:n], w[:, k, m * rows:(m + 1) * rows],
                                         act_in[:, k, 0:n], start=k == 0, stop=k == 1)
                last.then_inc(done, 1)

            def last_layer(s, q, static):
                nt = tiles_of(s, q, static)
                pe.wait_ge(u2_ready, s + q + 1)
                if static is None or static + q >= 1:
                    pe.wait_ge(y_ready, s + q)
                for t in range(nt):
                    for k in range(2):
                        last = pe.matmul(ps[:, 7, t * P:(t + 1) * P], u2[:, k, t * P:(t + 1) * P], wu3[:, k, :],
                                         start=k == 0, stop=k == 1)
                last.then_inc(u3_done, 1)

            def pe_step(s, par, has, static):
                if has(0):
                    transpose_nrm(s, par, static)
                if has(-1):
                    last_layer(s, -1, static)
                if has(2):
                    transpose_agg(s, 2, par, static)
                if has(0):
                    mlp_layer(s, static, nrmT_ready, z1_ready, 3, wu1, nrmT, H1, u1_done)
                if has(2):
                    product_msg(s, 2, static)
                if has(0):
                    mlp_layer(s, static, u1_ready, z2_ready, 5, wu2, u1, H2, u2_done)

            node_steps(pe, pe_step, -2, SUPERS)


def kernel(x, src, dst, edge_attr_5, L0_gnn_Wm1, L0_gnn_bm1, L0_gnn_Wm2, L0_gnn_bm2, L0_gnn_Wm3, L0_gnn_bm3,
           L0_gnn_ln_g, L0_gnn_ln_b, L0_gnn_Wu1, L0_gnn_bu1, L0_gnn_Wu2, L0_gnn_bu2, L0_gnn_Wu3, L0_gnn_bu3):
    import concourse.bacc as bacc
    from concourse.bass_utils import run_bass_kernel_spmd

    ea = np.zeros((R, EPAD), np.float32)
    ea[DE] = 1.0
    ea[:DE, :EDGES] = np.asarray(edge_attr_5).T
    ea = np.ascontiguousarray(ea.reshape(R, PIECES, PIECE).transpose(1, 0, 2)).reshape(PIECES, P, PC)
    dst_pad = np.full(EPAD, NODES, np.int32)
    dst_pad[:EDGES] = np.asarray(dst)

    def tr(w):
        return np.ascontiguousarray(np.asarray(w).T)

    arrays = {
        "ea": ea,
        "dst_t": tr(dst_pad.reshape(TILES, P)),
        "dst_g": dst_pad.reshape(GROUPS // 2, 2 * GE),
        "x": np.asarray(x),
        "wm1": np.asarray(L0_gnn_Wm1), "wm1t": tr(L0_gnn_Wm1), "bm1": np.asarray(L0_gnn_bm1),
        "wm2t": tr(L0_gnn_Wm2), "bm2": np.asarray(L0_gnn_bm2),
        "wm3t": tr(L0_gnn_Wm3), "bm3": np.asarray(L0_gnn_bm3),
        "ln_g": np.asarray(L0_gnn_ln_g), "ln_b": np.asarray(L0_gnn_ln_b),
        "wu1t": tr(L0_gnn_Wu1), "bu1": np.asarray(L0_gnn_bu1),
        "wu2t": tr(L0_gnn_Wu2), "bu2": np.asarray(L0_gnn_bu2),
        "wu3t": tr(L0_gnn_Wu3), "bu3": np.asarray(L0_gnn_bu3),
    }
    nc = bacc.Bacc("TRN2", target_bir_lowering=False, num_devices=1)
    args = [nc.dram_tensor(f"in_{k}", a.shape, mybir.dt.from_np(a.dtype), kind="ExternalInput").ap()
            for k, a in arrays.items()]
    out = nc.dram_tensor("out", (NODES, D), F32, kind="ExternalOutput").ap()
    gnn_kernel(nc, *args, out)
    r = run_bass_kernel_spmd(nc, [{f"in_{k}": a for k, a in arrays.items()}], core_ids=[0])
    return r.results[0]["out"]
```

```python
import concourse.bass as bass
from concourse import mybir
from contextlib import ExitStack
import numpy as np

F32 = mybir.dt.float32
F32R = mybir.dt.float32r
BF16 = mybir.dt.bfloat16
I32 = mybir.dt.int32
ALU = mybir.AluOpType
ACT = mybir.ActivationFunctionType
AX = mybir.AxisListType

NODES, EDGES, D, DE = 6250, 106250, 128, 5
U1, U2 = 214, 172
P = 128
GT = 4
GE = GT * P
PIECE = 8192
PIECES = -(-EDGES // PIECE)
EPAD = PIECES * PIECE
GROUPS = EPAD // GE
TILES = EPAD // P
R = DE + 1
K54 = 9 * R
PC = R * PIECE // P
CHUNK = 2048
CG = CHUNK // GE
BODY = 2 * CG
TURNS = GROUPS // BODY
PG = PIECE // GE
W = D + 1
WH = D + 2
WL = WH + D
WIN = 64
NT = -(-NODES // P)
LASTROWS = NODES - (NT - 1) * P
ST = 4
SUPERS = -(-NT // ST)
H1, H2 = U1 // 2, U2 // 2
NB = 7
SLOPE = 0.01
EPS = 1e-5


def gnn_kernel(nc, ea, dst_t, dst_g, x, wm1, wm1t, bm1, wm2t, bm2, wm3t, bm3, ln_g, ln_b,
               wu1t, bu1, wu2t, bu2, wu3t, bu3, out):
    ctx = ExitStack()
    with ctx:
        def sb(name, shape, dt=F32):
            return ctx.enter_context(nc.sbuf_tensor(name, shape, dt))

        def sem(name):
            return ctx.enter_context(nc.semaphore(name))

        parts_dram = nc.dram_tensor("parts_dram", [PIECES, K54, PIECE], BF16)
        wparts_dram = nc.dram_tensor("wparts_dram", [3 * R, 2 * D], BF16)
        meta_dram = nc.dram_tensor("meta_dram", [3, GROUPS], I32)

        ps = ctx.enter_context(nc.psum_tensor("ps", [P, 8, 512], F32))

        ident = sb("ident", [P, P])
        iota = sb("iota", [P, P])
        w1n = sb("w1n", [P, R])
        w1t = sb("w1t", [R, D])
        b2row = sb("b2row", [R, D])
        lin = sb("lin", [R, D])
        wres = sb("wres", [R, 2, D])
        wpart = sb("wpart", [R, 3, 2, D], BF16)
        w54 = sb("w54", [K54, 2, D], BF16)
        w2t = sb("w2t", [D, D])
        w3t = sb("w3t", [D, D])
        bm3b = sb("bm3b", [P, D])
        lng = sb("lng", [P, 2])
        lnb = sb("lnb", [P, 2])
        wu1 = sb("wu1", [P, 2, U1])
        wu2 = sb("wu2", [H1, 2, U2])
        wu3 = sb("wu3", [H2, 2, D])
        bu1c = sb("bu1c", [H1, 2])
        bu2c = sb("bu2c", [H2, 2])
        bu3b = sb("bu3b", [P, D])

        half = sb("half", [P, ST])
        eps = sb("eps", [P, ST])

        ea_sb = sb("ea_sb", [P, PC])
        zero_pc = sb("zero_pc", [P, PC])
        ea_part = sb("ea_part", [P, 3, PC], BF16)

        gmin = sb("gmin", [GROUPS // 2, 2], I32)
        gmax = sb("gmax", [GROUPS // 2, 2], I32)
        gpar = sb("gpar", [GROUPS // 2, 2], I32)
        ghalf = sb("ghalf", [GROUPS // 2, 2], I32)
        gmeta = sb("gmeta", [GROUPS // 2, 3, 2], I32)
        base_b = sb("base_b", [P, GROUPS], I32)
        slot_row = sb("slot_row", [1, GROUPS], I32)
        span_row = sb("span_row", [1, GROUPS], I32)
        span_max = sb("span_max", [1, 1], I32)
        flag = sb("flag", [1, 1], I32)
        dst_sb = sb("dst_sb", [P, TILES], I32)
        dst_rel = sb("dst_rel", [P, TILES])

        a54 = sb("a54", [K54, 2, CHUNK], BF16)
        shared = sb("shared", [P, 4, 2, GE])
        h1, relu2, h2 = (shared[:, n, :, :] for n in range(3))
        h2_parts = sb("h2_parts", [P, 4, GT, WL], F32R)
        onehot = sb("onehot", [P, 2, GE], F32R)
        acc = sb("acc", [P, 2, NT, W])

        shift = sb("shift", [P, NT, W])
        x_sb = sb("x_sb", [P, NT, D])
        xb = sb("xb", [P, 2, ST, D])
        agg = sb("agg", [P, 2, ST, W])
        aggT = sb("aggT", [P, ST * P])
        msg = sb("msg", [P, 2, ST, D])
        bn = sb("bn", [P, ST, 12])
        mv = sb("mv", [P, ST, 2])
        rstd = sb("rstd", [P, 2, ST])
        mrs = sb("mrs", [P, 2, ST])
        nrm = sb("nrm", [P, 2, ST, 2 * D])
        nrmT = sb("nrmT", [P, 2, ST * P])
        z1, u1 = (shared[0:H1, n, :, :] for n in range(2))
        z2, u2 = (shared[0:H2, n, :, :] for n in range(2, 4))
        y = sb("y", [P, 2, ST, D])
        ybn = sb("ybn", [P, ST, 6])
        ymv = sb("ymv", [P, ST, 2])
        yrstd = sb("yrstd", [P, 2, ST])
        ymrs = sb("ymrs", [P, 2, ST])
        o_sb = sb("o_sb", [P, 2, ST, D])
        gdst = shift[0:GROUPS // 2, :, :].rearrange("p a b -> p (a b)")[:, 0:2 * GE].bitcast(I32)\
            .rearrange("p (a e) -> p a e", a=2)
        node_iota = shift[:, :, :].rearrange("p a b -> p (a b)")[:, 0:NT * P]

        weights_in = sem("weights_in")
        late_in = sem("late_in")
        b2row_zero = sem("b2row_zero")
        b2row_in = sem("b2row_in")
        x_zero = sem("x_zero")
        ea_in = sem("ea_in")
        dst_in = sem("dst_in")
        consts = sem("consts")
        pool_ident = sem("pool_ident")
        lin_mm = sem("lin_mm")
        wsplit = sem("wsplit")
        w54_in = sem("w54_in")
        split_step = sem("split_step")
        parts_ready = sem("parts_ready")
        parts_out = sem("parts_out")
        wparts_out = sem("wparts_out")
        meta_step = sem("meta_step")
        meta_out = sem("meta_out")
        meta_in = sem("meta_in")
        rel_ready = sem("rel_ready")
        flag_ready = sem("flag_ready")
        ones_ready = sem("ones_ready")
        acc_zero = sem("acc_zero")

        chunk_in = [sem(f"chunk_in{n}") for n in range(2)]
        s1_done = sem("s1_done")
        h1_ready = sem("h1_ready")
        s2_done = sem("s2_done")
        relu2_ready = sem("relu2_ready")
        h2_ready = sem("h2_ready")
        hi_ready = sem("hi_ready")
        lo_ready = sem("lo_ready")
        acc_hi_done = sem("acc_hi_done")
        onehot_ready = sem("onehot_ready")
        s3_done = sem("s3_done")
        acc_done = sem("acc_done")

        g_tile_in = sem("g_tile_in")
        g_iota = sem("g_iota")
        g_s1_done = sem("g_s1_done")
        g_h1_ready = sem("g_h1_ready")
        g_s2_done = sem("g_s2_done")
        g_relu2_ready = sem("g_relu2_ready")
        g_h2_ready = sem("g_h2_ready")
        g_hi_ready = sem("g_hi_ready")
        g_lo_ready = sem("g_lo_ready")
        g_onehot = sem("g_onehot")
        g_s3_done = sem("g_s3_done")
        g_acc_done = sem("g_acc_done")

        edges_done = sem("edges_done")
        shift_in = [sem(f"shift_in{n}") for n in range(2)]
        agg_ready = sem("agg_ready")
        a1_done = sem("a1_done")
        aggT_ready = sem("aggT_ready")
        a2_done = sem("a2_done")
        stats_ready = sem("stats_ready")
        ystats_ready = sem("ystats_ready")
        msg_ready = sem("msg_ready")
        bn_ready = sem("bn_ready")
        rstd_step = sem("rstd_step")
        nrm_ready = sem("nrm_ready")
        xb_ready = sem("xb_ready")
        t_done = sem("t_done")
        nrmT_ready = sem("nrmT_ready")
        u1_done = sem("u1_done")
        z1_ready = sem("z1_ready")
        u1_ready = sem("u1_ready")
        u2_done = sem("u2_done")
        z2_ready = sem("z2_ready")
        u2_ready = sem("u2_ready")
        u3_done = sem("u3_done")
        y_ready = sem("y_ready")
        ybn_ready = sem("ybn_ready")
        yrstd_step = sem("yrstd_step")
        rstd_ready = sem("rstd_ready")
        yrstd_ready = sem("yrstd_ready")
        out_ready = sem("out_ready")
        out_stored = [sem(f"out_stored{n}") for n in range(2)]

        N_WEIGHTS, N_LATE = 5, 14

        def node_steps(eng, step, first, last):
            lo, hi = 3, 9
            for s in range(first, lo):
                step(s, s % 2, lambda q, s=s: 0 <= s + q < SUPERS, s)
            with eng.Fori(0, (hi - lo) // 2) as i:
                for j in range(2):
                    step(2 * i + lo + j, (lo + j) % 2, lambda q: True, None)
            for s in range(hi, last + 1):
                step(s, s % 2, lambda q, s=s: 0 <= s + q < SUPERS, s)

        def tiles_of(s, q, static):
            return ST if static is None or static + q < SUPERS - 1 else NT - ST * (SUPERS - 1)

        def from_tile(s, q):
            return (s + q) * ST

        block = ctx.enter_context(nc.Block())

        @block.sync
        def _(sp):
            sp.dma_start(ea_sb[:, :], ea[0]).then_inc(ea_in, 16)
            sp.dma_start(gdst[:, :, :], dst_g.rearrange("p (a e) -> p a e", a=2)).then_inc(dst_in, 16)
            sp.dma_start(dst_sb[:, :], dst_t).then_inc(dst_in, 16)

            def store_parts(q):
                sp.wait_ge(parts_ready, q + 1)
                for p in range(3):
                    rows = parts_dram[bass.ds(q, 1), 3 * R * p:3 * R * (p + 1), :]
                    sp.dma_start(rows.rearrange("q (rep r) n -> (q rep) (r n)", rep=3)
                                 .rearrange("rep (x c) -> x rep c", x=P),
                                 ea_part[:, p, :].unsqueeze(1).to_broadcast([P, 3, PC])).then_inc(parts_out, 16)

            def load_piece(q):
                sp.dma_start(ea_sb[:, :], ea[bass.ds(q, 1), :, :].rearrange("q p c -> (q p) c")).then_inc(ea_in, 16)

            sp.wait_ge(meta_step, 6)
            for kind in range(3):
                sp.dma_start(meta_dram[kind, :].rearrange("(p a) -> p a", a=2), gmeta[:, kind, :]).then_inc(meta_out, 16)
            store_parts(0)
            load_piece(1)
            sp.wait_ge(meta_out, 48)
            sp.dma_start(base_b[:, :], meta_dram[0, :].partition_broadcast(P)).then_inc(meta_in, 16)
            sp.dma_start(slot_row[:, :], meta_dram[1:2, :]).then_inc(meta_in, 16)
            sp.dma_start(span_row[:, :], meta_dram[2:3, :]).then_inc(meta_in, 16)

            def load_late():
                for dst, src in [
                    (w3t[:, :], wm3t), (bm3b[:, :], bm3.partition_broadcast(P)),
                    (wu1[:, :, :], wu1t.rearrange("(a p) m -> p a m", p=P)),
                    (wu2[:, :, :], wu2t.rearrange("(a p) m -> p a m", p=H1)),
                    (wu3[:, :, :], wu3t.rearrange("(a p) m -> p a m", p=H2)),
                    (bu3b[:, :], bu3.partition_broadcast(P)),
                ]:
                    sp.dma_start(dst, src).then_inc(late_in, 16)
                for dst, src, rows in [(lng, ln_g, P), (lnb, ln_b, P), (bu1c, bu1, H1), (bu2c, bu2, H2)]:
                    sp.dma_start(dst[:, :], src.rearrange("(a p) -> p a", p=rows),
                                 allow_slow_non_contiguous=True).then_inc(late_in, 16)
                for n in range(3):
                    a, b = n * (NT // 3), (n + 1) * (NT // 3)
                    sp.dma_start(x_sb[:, a:b, :], x[a * P:b * P, :].rearrange("(t p) f -> p t f", p=P)).then_inc(late_in, 16)
                sp.wait_ge(x_zero, 1)
                sp.dma_start(x_sb[0:LASTROWS, NT - 1, :], x[(NT - 1) * P:NODES, :]).then_inc(late_in, 16)

            sp.wait_ge(flag_ready, 1)
            general = sp.value_load(flag[0:1, 0:1], min_val=0, max_val=1)
            with sp.If(general < 1):
                def load_chunk(q, k, free):
                    if free:
                        sp.wait_ge(s2_done, q * PG + CG * (k - 1))
                    sp.dma_start(a54[:, k % 2, :], parts_dram[bass.ds(q, 1), :, k * CHUNK:(k + 1) * CHUNK]
                                 .rearrange("q r n -> (q r) n")).then_inc(chunk_in[k % 2], 16)

                def feed(q, first, store, load):
                    sp.wait_ge(parts_out, 48 * (q + 1))
                    load_chunk(q, 0, not first)
                    load_chunk(q, 1, not first)
                    load_chunk(q, 2, True)
                    if store:
                        store_parts(q + 1)
                    if load:
                        load_piece(q + 2)
                    load_chunk(q, 3, True)

                feed(0, True, True, True)
                load_late()
                with sp.Fori(1, PIECES - 2) as q:
                    feed(q, False, True, True)
                feed(PIECES - 2, False, True, False)
                feed(PIECES - 1, False, False, False)
            with sp.Else():
                load_late()
                with sp.Fori(1, PIECES - 1) as q:
                    store_parts(q)
                    load_piece(q + 1)
                store_parts(PIECES - 1)
                sp.wait_ge(parts_out, 48 * PIECES)
                with sp.Fori(0, PIECES) as q:
                    with sp.Fori(0, PIECE // P) as k:
                        sp.wait_ge(g_s2_done, q * (PIECE // P) + k + 1)
                        sp.dma_start(a54[:, 0, 0:P], parts_dram[bass.ds(q, 1), :, bass.ds(k * P, P)]
                                     .rearrange("q r n -> (q r) n")).then_inc(g_tile_in, 16)

            sp.wait_ge(edges_done, 1)
            for n, (a, b) in enumerate([(0, 2 * ST), (2 * ST, NT)]):
                lo = max(a, 1)
                sp.dma_start(shift[0:WIN, lo:b, :], acc[WIN:P, 1, lo - 1:b - 1, :]).then_inc(shift_in[n], 16)
                sp.dma_start(shift[WIN:P, a:b, :], acc[0:WIN, 1, a:b, :]).then_inc(shift_in[n], 16)

            for s in range(SUPERS):
                t0 = s * ST * P
                sp.wait_ge(out_ready, s + 1)
                if s < SUPERS - 1:
                    sp.dma_start(out[t0:t0 + ST * P, :].rearrange("(t p) f -> p t f", p=P), o_sb[:, s % 2, :, :])\
                        .then_inc(out_stored[s % 2], 16)
                else:
                    sp.dma_start(out[t0:NODES, :], o_sb[0:LASTROWS, s % 2, 0, :]).then_inc(out_stored[s % 2], 16)
            sp.wait_ge(out_stored[0], 16 * ((SUPERS + 1) // 2))
            sp.wait_ge(out_stored[1], 16 * (SUPERS // 2))

        @block.scalar
        def _(act):
            act.dma_start(w1n[:, 0:DE], wm1).then_inc(weights_in, 16)
            act.dma_start(w1n[:, DE:R], bm1.rearrange("(p a) -> p a", a=1)).then_inc(weights_in, 16)
            act.dma_start(w1t[0:DE, :], wm1t).then_inc(weights_in, 16)
            act.dma_start(w1t[DE:R, :], bm1.rearrange("(a p) -> a p", a=1)).then_inc(weights_in, 16)
            act.dma_start(w2t[:, :], wm2t).then_inc(weights_in, 16)
            act.wait_ge(b2row_zero, 1)
            act.dma_start(b2row[DE:R, :], bm2.rearrange("(a p) -> a p", a=1)).then_inc(b2row_in, 16)

            act.wait_ge(wsplit, 6)
            act.dma_start(wparts_dram.ap().rearrange("(k r) n -> r k n", r=R),
                          wpart[:, :, :, :].rearrange("r k h n -> r k (h n)")).then_inc(wparts_out, 16)
            act.wait_ge(wparts_out, 16)
            act.dma_start(w54[:, :, :].rearrange("k h n -> k (h n)"),
                          wparts_dram.ap().partition_broadcast(3)).then_inc(w54_in, 16)

            act.wait_ge(flag_ready, 1)
            general = act.value_load(flag[0:1, 0:1], min_val=0, max_val=1)
            with act.If(general < 1):
                def first_relu(g, j, peeled):
                    act.wait_ge(s1_done, g + 1)
                    if not (peeled and g < 2):
                        act.wait_ge(s2_done, g - 1)
                    act.activation(h1[:, j % 2, :], ps[:, j % 2, :], ACT.Relu, scale=1.0 - SLOPE).then_inc(h1_ready, 1)

                def second_relu(g, j, peeled):
                    act.wait_ge(s2_done, g + 1)
                    if not (peeled and g < 2):
                        act.wait_ge(h2_ready, g - 1)
                    act.activation(relu2[:, j % 2, :], ps[:, 2 + j % 2, :], ACT.Relu, scale=1.0 - SLOPE)\
                        .then_inc(relu2_ready, 1)

                def high_part(g, j, peeled):
                    act.wait_ge(h2_ready, g + 1)
                    if not (peeled and g < 4):
                        act.wait_ge(s3_done, g - 3)
                    act.activation(h2_parts[:, j % 4, :, 0:D], h2[:, j % 2, :].rearrange("p (t f) -> p t f", t=GT),
                                   ACT.Copy).then_inc(hi_ready, 1)

                def act_edge_step(s, j, peeled):
                    first_relu(s, j, peeled)
                    if not (peeled and s < 2):
                        high_part(s - 2, (j - 2) % BODY, peeled)
                    if not (peeled and s < 1):
                        second_relu(s - 1, (j - 1) % BODY, peeled)

                for j in range(BODY):
                    act_edge_step(j, j, True)
                with act.Fori(1, TURNS) as i:
                    for j in range(BODY):
                        act_edge_step(i * BODY + j, j, False)
                high_part(GROUPS - 2, BODY - 2, True)
                second_relu(GROUPS - 1, BODY - 1, True)
                high_part(GROUPS - 1, BODY - 1, True)
            with act.Else():
                with act.Fori(0, TILES) as t:
                    act.wait_ge(g_s1_done, t + 1)
                    act.activation(h1[:, 0, 0:P], ps[:, 0, 0:P], ACT.Relu, scale=1.0 - SLOPE).then_inc(g_h1_ready, 1)
                    act.wait_ge(g_s2_done, t + 2)
                    act.activation(relu2[:, 0, 0:P], ps[:, 1, 0:P], ACT.Relu, scale=1.0 - SLOPE).then_inc(g_relu2_ready, 1)
                    act.wait_ge(g_h2_ready, t + 1)
                    act.activation(h2_parts[:, 0, 0, 0:D], h2[:, 0, 0:P], ACT.Copy).then_inc(g_hi_ready, 1)

            act.wait_ge(late_in, 16 * N_LATE)

            def copy_aggT(s, q, static):
                nt = tiles_of(s, q, static)
                act.wait_ge(a1_done, s + q + 1)
                if static is None or static + q >= 1:
                    act.wait_ge(a2_done, s + q)
                act.activation(aggT[:, 0:nt * P], ps[:, 0, 0:nt * P], ACT.Copy).then_inc(aggT_ready, 1)

            def scale_nrmT(s, static):
                n = tiles_of(s, 0, static) * P
                if static is None or static >= 1:
                    act.wait_ge(u1_done, 2 * s)
                for h in range(2):
                    act.wait_ge(t_done, 2 * s + h + 1)
                    act.activation(nrmT[:, h, 0:n], ps[:, 1 + h, 0:n], ACT.Identity,
                                   bias=lnb[:, h:h + 1], scale=lng[:, h:h + 1]).then_inc(nrmT_ready, 1)

            def add_bias(s, static, done, read, z, bank, bias, rows, ready):
                n = tiles_of(s, 0, static) * P
                for h in range(2):
                    act.wait_ge(done, 2 * s + h + 1)
                    if static is None or static >= 1:
                        act.wait_ge(read, 2 * s + h - 1)
                    act.activation(z[:, h, 0:n], ps[0:rows, bank + h, 0:n], ACT.Identity, bias=bias[:, h:h + 1])\
                        .then_inc(ready, 1)

            def normalise(s, q, par, static, half_):
                nt = tiles_of(s, q, static)
                t0 = from_tile(s, q)
                b = (par + q) % 2
                if half_ == 0:
                    act.wait_ge(rstd_ready, s + q + 1)
                    if static is None or static + q >= 2:
                        act.wait_ge(t_done, 2 * (s + q - 1))
                for t in range(nt):
                    src = msg[:, b, t, :] if half_ else x_sb[:, bass.ds(t0 + t, 1), :].rearrange("p a f -> p (a f)")
                    last = act.activation(nrm[:, b, t, half_ * D:(half_ + 1) * D], src, ACT.Identity,
                                          bias=mrs[:, b, t:t + 1], scale=rstd[:, b, t:t + 1])
                last.then_inc(nrm_ready, 1)

            def finish(s, q, par, static):
                nt = tiles_of(s, q, static)
                b = 1 - par
                act.wait_ge(yrstd_ready, s + q + 1)
                if static is None:
                    act.wait_ge(out_stored[b], (s + q - b) * 8)
                elif static + q >= 2:
                    act.wait_ge(out_stored[b], 16 * ((static + q - b) // 2))
                for t in range(nt):
                    last = act.activation(o_sb[:, b, t, :], y[:, b, t, :], ACT.Identity,
                                          bias=ymrs[:, b, t:t + 1], scale=yrstd[:, b, t:t + 1])
                last.then_inc(out_ready, 1)

            def act_step(s, par, has, static):
                if has(0):
                    scale_nrmT(s, static)
                if has(2):
                    copy_aggT(s, 2, static)
                if has(1):
                    normalise(s, 1, par, static, 0)
                if has(0):
                    add_bias(s, static, u1_done, u1_ready, z1, 3, bu1c, H1, z1_ready)
                if has(-1):
                    finish(s, -1, par, static)
                if has(1):
                    normalise(s, 1, par, static, 1)
                if has(0):
                    add_bias(s, static, u2_done, u2_ready, z2, 5, bu2c, H2, z2_ready)

            node_steps(act, act_step, -2, SUPERS)

        @block.gpsimd
        def _(pool):
            pool.memset(b2row[:, :], 0.0).then_inc(b2row_zero, 1)
            pool.iota(iota[:, :], pattern=[[1, P]], base=0, channel_multiplier=0,
                      allow_small_or_imprecise_dtypes=True).then_inc(consts, 1)
            pool.memset(zero_pc[:, :], 0.0).then_inc(split_step, 1)

            def split_quarter(q, n, first):
                pool.wait_ge(split_step, 3 * q + n + 1)
                if n == 0:
                    pool.wait_ge(ea_in, 16 * (q + 1))
                    if not first:
                        pool.wait_ge(parts_out, 48 * q)
                    pool.tensor_tensor(ea_part[:, 0, :], ea_sb[:, :], zero_pc[:, :], ALU.add).then_inc(split_step, 1)
                elif n == 1:
                    pool.tensor_tensor(ea_sb[:, :], ea_sb[:, :], ea_part[:, 0, :], ALU.subtract).then_inc(split_step, 1)
                elif n == 2:
                    pool.tensor_tensor(ea_part[:, 1, :], ea_sb[:, :], zero_pc[:, :], ALU.add).then_inc(split_step, 1)
                else:
                    pool.tensor_tensor(ea_part[:, 2, :], ea_sb[:, :], ea_part[:, 1, :], ALU.subtract).then_inc(parts_ready, 1)

            def split_piece(q, first):
                for n in range(4):
                    split_quarter(q, n, first)

            split_piece(0, True)
            pool.memset(h2_parts[:, :, :, D:D + 1].bitcast(F32), 1.0).then_inc(ones_ready, 1)
            pool.memset(h2_parts[:, :, :, D + 1:WH].bitcast(F32), 0.0).then_inc(ones_ready, 1)
            pool.memset(x_sb[:, NT - 1, :], 0.0).then_inc(x_zero, 1)
            pool.memset(ident[:, :], 0.0).then_inc(pool_ident, 1)
            pool.wait_ge(pool_ident, 1)
            pool.affine_select(out=ident[:, :], in_=ident[:, :], compare_op=ALU.not_equal, fill=1.0,
                               base=0, pattern=[[-1, P]], channel_multiplier=1).then_inc(pool_ident, 1)

            pool.memset(half[:, :], -0.5).then_inc(consts, 1)
            pool.memset(eps[:, :], EPS).then_inc(consts, 1)
            pool.memset(acc[:, 1, :, :], 0.0).then_inc(acc_zero, 1)
            pool.memset(acc[:, 0, NT // 2:NT, :], 0.0).then_inc(acc_zero, 1)

            pool.wait_ge(flag_ready, 1)
            general = pool.value_load(flag[0:1, 0:1], min_val=0, max_val=1)

            with pool.If(general < 1):
                def low_part(g, j):
                    pool.wait_ge(hi_ready, g + 1)
                    pool.tensor_tensor(h2_parts[:, j % 4, :, WH:WL], h2[:, j % 2, :].rearrange("p (t f) -> p t f", t=GT),
                                       h2_parts[:, j % 4, :, 0:D].bitcast(F32), ALU.subtract).then_inc(lo_ready, 1)

                def piece_turn(q, split):
                    for j in range(PG):
                        if split and j % 2 == 0 and j < 8:
                            split_quarter(q + 1, j // 2, False)
                        low_part(q * PG + j, j)

                piece_turn(0, True)
                with pool.Fori(1, PIECES - 1) as q:
                    piece_turn(q, True)
                piece_turn(PIECES - 1, False)
            with pool.Else():
                pool.iota(node_iota, pattern=[[1, NT * P]], base=0, channel_multiplier=0,
                          allow_small_or_imprecise_dtypes=True).then_inc(g_iota, 1)
                with pool.Fori(1, PIECES) as q:
                    split_piece(q, False)
                with pool.Fori(0, TILES) as t:
                    pool.wait_ge(g_hi_ready, t + 1)
                    pool.tensor_tensor(h2_parts[:, 0, 0, WH:WL], h2[:, 0, 0:P], h2_parts[:, 0, 0, 0:D].bitcast(F32),
                                       ALU.subtract).then_inc(g_lo_ready, 1)

            pool.wait_ge(late_in, 16 * N_LATE)
            pool.wait_ge(consts, 3)

            def add_bu3(s, par, static):
                nt = tiles_of(s, 0, static)
                if static is None or static >= 2:
                    pool.wait_ge(y_ready, s - 1)
                pool.tensor_tensor(xb[:, par, 0:nt, :], x_sb[:, bass.ds(from_tile(s, 0), nt), :],
                                   bu3b[:, :].unsqueeze(1).to_broadcast([P, nt, D]), ALU.add).then_inc(xb_ready, 1)

            def scales(n, nt, b, ready, step, used, used_per, used_from, mv_, r, m, done):
                pool.wait_ge(ready, n + 1)
                if used_from:
                    pool.wait_ge(used, (n - 1) * used_per)
                pool.tensor_tensor(r[:, b, 0:nt], mv_[:, 0:nt, 1], eps[:, 0:nt], ALU.add).then_inc(step, 1)
                pool.tensor_scalar(m[:, b, 0:nt], mv_[:, 0:nt, 0], -1.0, None, ALU.mult).then_inc(step, 1)
                pool.wait_ge(step, 3 * n + 2)
                pool.tensor_tensor(r[:, b, 0:nt], r[:, b, 0:nt], half[:, 0:nt], ALU.pow).then_inc(step, 1)
                pool.wait_ge(step, 3 * n + 3)
                pool.tensor_tensor(m[:, b, 0:nt], m[:, b, 0:nt], r[:, b, 0:nt], ALU.mult).then_inc(done, 1)

            def pool_step(s, par, has, static):
                if has(-1):
                    scales(s - 1, tiles_of(s, -1, static), 1 - par, ystats_ready, yrstd_step, out_ready, 1,
                           static is None or static >= 3, ymv, yrstd, ymrs, yrstd_ready)
                if has(2):
                    scales(s + 2, tiles_of(s, 2, static), par, stats_ready, rstd_step, nrm_ready, 2,
                           static is None or static >= 0, mv, rstd, mrs, rstd_ready)
                if has(0):
                    add_bu3(s, par, static)

            node_steps(pool, pool_step, -2, SUPERS)

        @block.vector
        def _(dve):
            dve.wait_ge(dst_in, 32)
            dve.tensor_reduce(gmin[:, :], gdst[:, :, :], AX.X, ALU.min).then_inc(meta_step, 1)
            dve.tensor_reduce(gmax[:, :], gdst[:, :, :], AX.X, ALU.max).then_inc(meta_step, 1)
            dve.wait_ge(meta_step, 2)
            dve.tensor_scalar(gmeta[:, 0, :], gmin[:, :], -WIN, None, ALU.bitwise_and).then_inc(meta_step, 1)
            dve.tensor_scalar(gpar[:, :], gmin[:, :], 6, 1, ALU.logical_shift_right, ALU.bitwise_and)
            dve.tensor_scalar(ghalf[:, :], gmin[:, :], 7, None, ALU.logical_shift_right).then_inc(meta_step, 1)
            dve.wait_ge(meta_step, 4)
            dve.tensor_tensor(gmeta[:, 2, :], gmax[:, :], gmeta[:, 0, :], ALU.subtract).then_inc(meta_step, 1)
            dve.scalar_tensor_tensor(out=gmeta[:, 1, :], in0=gpar[:, :], scalar=float(NT), in1=ghalf[:, :],
                                     op0=ALU.mult, op1=ALU.add).then_inc(meta_step, 1)

            dve.wait_ge(lin_mm, 1)
            dve.wait_ge(b2row_in, 16)
            dve.scalar_tensor_tensor(out=wres[:, 1, :], in0=ps[0:R, 7, 0:D], scalar=SLOPE, in1=b2row[:, :],
                                     op0=ALU.mult, op1=ALU.add)
            dve.tensor_copy(wres[:, 0, :], w1t[:, :]).then_inc(wsplit, 1)
            dve.wait_ge(wsplit, 1)
            for part in range(3):
                dve.tensor_copy(wpart[:, part, :, :], wres[:, :, :]).then_inc(wsplit, 1)
                if part < 2:
                    dve.wait_ge(wsplit, 2 + 2 * part)
                    dve.tensor_tensor(wres[:, :, :], wres[:, :, :], wpart[:, part, :, :], ALU.subtract).then_inc(wsplit, 1)
                    dve.wait_ge(wsplit, 3 + 2 * part)

            dve.memset(acc[:, 0, 0:NT // 2, :], 0.0).then_inc(acc_zero, 1)
            dve.wait_ge(meta_in, 48)
            dve.tensor_reduce(span_max[:, :], span_row[:, :], AX.X, ALU.max).then_inc(meta_step, 1)
            dve.wait_ge(meta_step, 7)
            dve.tensor_scalar(flag[:, :], span_max[:, :], float(P), None, ALU.is_ge).then_inc(flag_ready, 1)
            dve.tensor_tensor(dst_rel[:, :].rearrange("p (g t) -> p g t", t=GT),
                              dst_sb[:, :].rearrange("p (g t) -> p g t", t=GT),
                              base_b[:, :].unsqueeze(2).to_broadcast([P, GROUPS, GT]),
                              ALU.subtract).then_inc(rel_ready, 1)

            dve.wait_ge(acc_zero, 3)
            dve.wait_ge(rel_ready, 1)
            dve.wait_ge(consts, 1)
            dve.wait_ge(flag_ready, 1)
            general = dve.value_load(flag[0:1, 0:1], min_val=0, max_val=1)

            def leaky(out_, in_):
                return dve.scalar_tensor_tensor(out=out_, in0=in_, scalar=SLOPE, in1=in_, op0=ALU.mult, op1=ALU.max)

            def leaky_sum(out_, z, relu):
                return dve.scalar_tensor_tensor(out=out_, in0=z, scalar=SLOPE, in1=relu, op0=ALU.mult, op1=ALU.add)

            with dve.If(general < 1):
                def second_leaky(g, j, peeled):
                    dve.wait_ge(relu2_ready, g + 1)
                    if not (peeled and g < 2):
                        dve.wait_ge(lo_ready, g - 1)
                    leaky_sum(h2[:, j % 2, :], ps[:, 2 + j % 2, :], relu2[:, j % 2, :]).then_inc(h2_ready, 1)

                def make_onehot(g, j, peeled):
                    if not (peeled and g < 2):
                        dve.wait_ge(s3_done, g - 1)
                    dve.tensor_tensor(onehot[:, j % 2, :].rearrange("p (t n) -> p t n", n=P),
                                      iota[:, :].unsqueeze(1).to_broadcast([P, GT, P]),
                                      dst_rel[:, bass.ds(g * GT, GT)].unsqueeze(2).to_broadcast([P, GT, P]),
                                      ALU.is_equal).then_inc(onehot_ready, 1)

                def window(g):
                    slot = dve.value_load(slot_row[0:1, bass.ds(g, 1)], min_val=0, max_val=2 * NT - 1)
                    return acc[:, :, :, :].rearrange("p a b c -> p (a b) c")[:, bass.ds(slot, 1), :]\
                        .rearrange("p a c -> p (a c)")

                def add_high(g, j, peeled, dst):
                    dve.wait_ge(s3_done, g + 1)
                    if not (peeled and g < 1):
                        dve.wait_ge(acc_done, g)
                    dve.tensor_tensor(dst, ps[:, 4 + j % 2, 0:W], dst, ALU.add).then_inc(acc_hi_done, 1)

                def add_low(g, j, dst):
                    dve.wait_ge(acc_hi_done, g + 1)
                    dst = dst[:, 0:D]
                    dve.tensor_tensor(dst, ps[:, 4 + j % 2, WH:WL], dst, ALU.add).then_inc(acc_done, 1)

                LAG = 5

                def dve_edge_step(s, j, peeled, last=False):
                    adds = not (peeled and s < LAG)
                    if adds:
                        dst = window(s - LAG)
                        add_high(s - LAG, (j - LAG) % BODY, peeled, dst)
                    if not (peeled and s < 1) and not (last and s - 1 >= GROUPS):
                        second_leaky(s - 1, (j - 1) % BODY, peeled)
                    if adds:
                        add_low(s - LAG, (j - LAG) % BODY, dst)
                    if not (peeled and s < 2) and not (last and s - 2 >= GROUPS):
                        make_onehot(s - 2, (j - 2) % BODY, peeled)

                for j in range(BODY):
                    dve_edge_step(j, j, True)
                with dve.Fori(1, TURNS) as i:
                    for j in range(BODY):
                        dve_edge_step(i * BODY + j, j, False)
                for j in range(LAG):
                    dve_edge_step(GROUPS + j, j, True, True)
                dve.wait_ge(acc_done, GROUPS)
            with dve.Else():
                dve.wait_ge(g_iota, 1)
                with dve.Fori(0, TILES) as t:
                    dve.wait_ge(g_relu2_ready, t + 1)
                    leaky_sum(h2[:, 0, 0:P], ps[:, 1, 0:P], relu2[:, 0, 0:P]).then_inc(g_h2_ready, 1)
                    for w in range(NB):
                        n = t * NB + w
                        dve.tensor_scalar(onehot[:, :, :].rearrange("p a b -> p (a b)")[:, 0:NB * P],
                                          node_iota[:, w * NB * P:(w + 1) * NB * P],
                                          dst_sb[:, bass.ds(t, 1)], None, ALU.is_equal).then_inc(g_onehot, 1)
                        dve.wait_ge(g_s3_done, n + 1)
                        for bank, (a, b) in enumerate([(0, 3), (3, 6), (6, NB)]):
                            dst = acc[:, 0, w * NB + a:w * NB + b, :]
                            last = dve.tensor_tensor(
                                dst, ps[:, 2 + bank, 0:(b - a) * WH].rearrange("p (a c) -> p a c", c=WH)[:, :, 0:W],
                                dst, ALU.add)
                        last.then_inc(g_acc_done, 1)
                        dve.wait_ge(g_acc_done, n + 1)
            dve.memset(shift[0:WIN, 0, :], 0.0).then_inc(edges_done, 1)
            dve.wait_ge(late_in, 16 * N_LATE)
            dve.wait_ge(shift_in[0], 32)
            dve.wait_ge(edges_done, 1)

            def gather(s, q, par, static):
                nt = tiles_of(s, q, static)
                t0 = from_tile(s, q)
                b = 1 - par
                if static is not None and static + q == 2:
                    dve.wait_ge(shift_in[1], 32)
                if static is None or static + q >= 2:
                    dve.wait_ge(a1_done, s + q - 1)
                dve.tensor_tensor(agg[:, b, 0:nt, :], acc[:, 0, bass.ds(t0, nt), :], shift[:, bass.ds(t0, nt), :],
                                  ALU.add).then_inc(agg_ready, 1)

            def x_stats(s, q, static):
                nt = tiles_of(s, q, static)
                t0 = from_tile(s, q)
                if static is None or static + q >= 1:
                    dve.wait_ge(stats_ready, s + q)
                for t in range(nt):
                    dve.bn_stats(bn[:, t, 0:6], x_sb[:, bass.ds(t0 + t, 1), :].rearrange("p a f -> p (a f)"))

            def messages(s, q, par, static):
                nt = tiles_of(s, q, static)
                b = par
                dve.wait_ge(a2_done, s + q + 1)
                dve.wait_ge(agg_ready, s + q + 1)
                if static is None or static + q >= 2:
                    dve.wait_ge(nrm_ready, 2 * (s + q - 1))
                if static is None or static + q >= 1:
                    dve.wait_ge(rstd_ready, s + q)
                for t in range(nt):
                    last = dve.scalar_tensor_tensor(out=msg[:, b, t, :], in0=bm3b[:, :], scalar=agg[:, b, t, D:W],
                                                    in1=ps[:, 0, t * P:(t + 1) * P], op0=ALU.mult, op1=ALU.add)
                last.then_inc(msg_ready, 1)
                dve.wait_ge(msg_ready, s + q + 1)
                for t in range(nt):
                    last = dve.bn_stats(bn[:, t, 6:12], msg[:, b, t, :])
                last.then_inc(bn_ready, 1)

            def moments(s, q, par, static):
                nt = tiles_of(s, q, static)
                for t in range(nt):
                    last = dve.bn_aggr(mv[:, t, :], bn[:, t, :])
                last.then_inc(stats_ready, 1)

            def mlp_leaky(s, static, z_ready, read, read_per, u, z, ready):
                n = tiles_of(s, 0, static) * P
                for h in range(2):
                    if h == 0 and (static is None or static >= 1):
                        dve.wait_ge(read, read_per * s)
                    dve.wait_ge(z_ready, 2 * s + h + 1)
                    leaky(u[:, h, 0:n], z[:, h, 0:n]).then_inc(ready, 1)

            def residual(s, q, par, static):
                nt = tiles_of(s, q, static)
                b = 1 - par
                dve.wait_ge(u3_done, s + q + 1)
                dve.wait_ge(xb_ready, s + q + 1)
                if static is None or static + q >= 2:
                    dve.wait_ge(out_ready, s + q - 1)
                dve.tensor_tensor(y[:, b, 0:nt, :], ps[:, 7, 0:nt * P].rearrange("p (t f) -> p t f", f=D),
                                  xb[:, b, 0:nt, :], ALU.add).then_inc(y_ready, 1)
                if static is None or static + q >= 1:
                    dve.wait_ge(yrstd_ready, s + q)
                dve.wait_ge(y_ready, s + q + 1)
                for t in range(nt):
                    last = dve.bn_stats(ybn[:, t, :], y[:, b, t, :])
                last.then_inc(ybn_ready, 1)


            def y_moments(s, q, par, static):
                nt = tiles_of(s, q, static)
                for t in range(nt):
                    last = dve.bn_aggr(ymv[:, t, :], ybn[:, t, :])
                last.then_inc(ystats_ready, 1)

            def dve_step(s, par, has, static):
                if has(-1):
                    residual(s, -1, par, static)
                    dve.wait_ge(ybn_ready, s)
                if has(2):
                    x_stats(s, 2, static)
                if has(-1):
                    y_moments(s, -1, par, static)
                if has(0):
                    mlp_leaky(s, static, z1_ready, u2_done, 2, u1, z1, u1_ready)
                if has(2):
                    messages(s, 2, par, static)
                    dve.wait_ge(bn_ready, s + 3)
                if has(3):
                    gather(s, 3, par, static)
                if has(2):
                    moments(s, 2, par, static)
                if has(0):
                    mlp_leaky(s, static, z2_ready, u3_done, 1, u2, z2, u2_ready)

            node_steps(dve, dve_step, -3, SUPERS)

        @block.tensor
        def _(pe):
            pe.wait_ge(weights_in, 16 * N_WEIGHTS)
            pe.matmul(ps[0:R, 7, 0:D], w1n[:, :], w2t[:, :], start=True, stop=True).then_inc(lin_mm, 1)
            pe.wait_ge(w54_in, 16)
            pe.wait_ge(flag_ready, 1)
            general = pe.value_load(flag[0:1, 0:1], min_val=0, max_val=1)
            with pe.If(general < 1):
                def layer1(g, j, turn, peeled):
                    if j % CG == 0:
                        pe.wait_ge(chunk_in[j // CG], 16 * (turn + 1))
                    if not (peeled and g < 2):
                        pe.wait_ge(h1_ready, g - 1)
                    e0 = (j % CG) * GE
                    pe.matmul(ps[:, j % 2, :], w54[:, 0, :], a54[:, j // CG, e0:e0 + GE],
                              start=True, stop=True).then_inc(s1_done, 1)

                def layer2(g, j, peeled):
                    pe.wait_ge(h1_ready, g + 1)
                    if not (peeled and g < 2):
                        pe.wait_ge(h2_ready, g - 1)
                    for t in range(GT):
                        e0 = (j % CG) * GE + t * P
                        pe.matmul(ps[:, 2 + j % 2, t * P:(t + 1) * P], a54[:, j // CG, e0:e0 + P], w54[:, 1, :],
                                  start=t == 0, stop=False, skip_group_check=True)
                    for t in range(GT):
                        last = pe.matmul(ps[:, 2 + j % 2, t * P:(t + 1) * P], h1[:, j % 2, t * P:(t + 1) * P],
                                         w2t[:, :], start=False, stop=True, skip_group_check=True)
                    last.then_inc(s2_done, 1)

                def edge_sum(g, j, peeled):
                    pe.wait_ge(lo_ready, g + 1)
                    pe.wait_ge(onehot_ready, g + 1)
                    if not (peeled and g < 2):
                        pe.wait_ge(acc_done, g - 1)
                    for t in range(GT):
                        last = pe.matmul(ps[:, 4 + j % 2, 0:WL], onehot[:, j % 2, t * P:(t + 1) * P],
                                         h2_parts[:, j % 4, t, :], start=t == 0, stop=t == GT - 1)
                    last.then_inc(s3_done, 1)

                LAG = 4

                def pe_edge_step(s, j, turn, peeled, last=False):
                    if not last:
                        layer1(s, j, turn, peeled)
                    if not (peeled and s < 1) and not (last and s - 1 >= GROUPS):
                        layer2(s - 1, (j - 1) % BODY, peeled)
                    if not (peeled and s < LAG):
                        edge_sum(s - LAG, (j - LAG) % BODY, peeled)

                pe.wait_ge(ones_ready, 2)
                for j in range(BODY):
                    pe_edge_step(j, j, 0, True)
                with pe.Fori(1, TURNS) as i:
                    for j in range(BODY):
                        pe_edge_step(i * BODY + j, j, i, False)
                for j in range(LAG):
                    pe_edge_step(GROUPS + j, j, None, True, True)
            with pe.Else():
                pe.wait_ge(ones_ready, 2)
                pe.sem_inc(g_s2_done, 1)
                with pe.Fori(0, TILES) as t:
                    pe.wait_ge(g_tile_in, 16 * (t + 1))
                    pe.matmul(ps[:, 0, 0:P], w54[:, 0, :], a54[:, 0, 0:P], start=True, stop=True).then_inc(g_s1_done, 1)
                    pe.wait_ge(g_h1_ready, t + 1)
                    pe.matmul(ps[:, 1, 0:P], a54[:, 0, 0:P], w54[:, 1, :], start=True, stop=False)
                    pe.matmul(ps[:, 1, 0:P], h1[:, 0, 0:P], w2t[:, :], start=False, stop=True).then_inc(g_s2_done, 1)
                    pe.wait_ge(g_lo_ready, t + 1)
                    for w in range(NB):
                        pe.wait_ge(g_onehot, t * NB + w + 1)
                        for k in range(NB):
                            c0 = (k % 3) * WH
                            hot = onehot[:, k * P // GE, k * P % GE:k * P % GE + P]
                            pe.matmul(ps[:, 2 + k // 3, c0:c0 + WH], hot, h2_parts[:, 0, 0, 0:WH], start=True, stop=False)
                            last = pe.matmul(ps[:, 2 + k // 3, c0:c0 + D], hot, h2_parts[:, 0, 0, WH:WL],
                                             start=False, stop=True)
                        last.then_inc(g_s3_done, 1)

            pe.wait_ge(pool_ident, 2)
            pe.wait_ge(late_in, 16 * N_LATE)

            def transpose_agg(s, q, par, static):
                nt = tiles_of(s, q, static)
                pe.wait_ge(agg_ready, s + q + 1)
                if static is None or static + q >= 1:
                    pe.wait_ge(msg_ready, s + q)
                for t in range(nt):
                    last = pe.transpose(ps[:, 0, t * P:(t + 1) * P], agg[:, par, t, 0:D], ident[:, :])
                last.then_inc(a1_done, 1)

            def product_msg(s, q, static):
                nt = tiles_of(s, q, static)
                pe.wait_ge(aggT_ready, s + q + 1)
                for t in range(nt):
                    last = pe.matmul(ps[:, 0, t * P:(t + 1) * P], aggT[:, t * P:(t + 1) * P], w3t[:, :],
                                     start=True, stop=True)
                last.then_inc(a2_done, 1)

            def transpose_nrm(s, par, static):
                nt = tiles_of(s, 0, static)
                pe.wait_ge(nrm_ready, 2 * (s + 1))
                if static is None or static >= 1:
                    pe.wait_ge(nrmT_ready, 2 * s)
                for h in range(2):
                    for t in range(nt):
                        last = pe.transpose(ps[:, 1 + h, t * P:(t + 1) * P], nrm[:, par, t, h * D:(h + 1) * D], ident[:, :])
                    last.then_inc(t_done, 1)

            def mlp_layer(s, static, in_ready, read, bank, w, act_in, rows, done):
                n = tiles_of(s, 0, static) * P
                if static is None or static >= 1:
                    pe.wait_ge(read, 2 * s)
                for k in range(2):
                    pe.wait_ge(in_ready, 2 * s + k + 1)
                    for m in range(2):
                        last = pe.matmul(ps[0:rows, bank + m, 0:n], w[:, k, m * rows:(m + 1) * rows],
                                         act_in[:, k, 0:n], start=k == 0, stop=k == 1)
                        if k == 1:
                            last.then_inc(done, 1)

            def last_layer(s, q, static):
                nt = tiles_of(s, q, static)
                if static is None or static + q >= 1:
                    pe.wait_ge(y_ready, s + q)
                for k in range(2):
                    pe.wait_ge(u2_ready, 2 * (s + q) + k + 1)
                    for t in range(nt):
                        last = pe.matmul(ps[:, 7, t * P:(t + 1) * P], u2[:, k, t * P:(t + 1) * P], wu3[:, k, :],
                                         start=k == 0 and t == 0, stop=k == 1, skip_group_check=True)
                last.then_inc(u3_done, 1)

            def pe_step(s, par, has, static):
                if has(0):
                    transpose_nrm(s, par, static)
                if has(-1):
                    last_layer(s, -1, static)
                if has(2):
                    transpose_agg(s, 2, par, static)
                if has(0):
                    mlp_layer(s, static, nrmT_ready, z1_ready, 3, wu1, nrmT, H1, u1_done)
                if has(2):
                    product_msg(s, 2, static)
                if has(0):
                    mlp_layer(s, static, u1_ready, z2_ready, 5, wu2, u1, H2, u2_done)

            node_steps(pe, pe_step, -2, SUPERS)


def kernel(x, src, dst, edge_attr_5, L0_gnn_Wm1, L0_gnn_bm1, L0_gnn_Wm2, L0_gnn_bm2, L0_gnn_Wm3, L0_gnn_bm3,
           L0_gnn_ln_g, L0_gnn_ln_b, L0_gnn_Wu1, L0_gnn_bu1, L0_gnn_Wu2, L0_gnn_bu2, L0_gnn_Wu3, L0_gnn_bu3):
    import concourse.bacc as bacc
    from concourse.bass_utils import run_bass_kernel_spmd

    ea = np.zeros((R, EPAD), np.float32)
    ea[DE] = 1.0
    ea[:DE, :EDGES] = np.asarray(edge_attr_5).T
    ea = np.ascontiguousarray(ea.reshape(R, PIECES, PIECE).transpose(1, 0, 2)).reshape(PIECES, P, PC)
    dst_pad = np.full(EPAD, NODES, np.int32)
    dst_pad[:EDGES] = np.asarray(dst)

    def tr(w):
        return np.ascontiguousarray(np.asarray(w).T)

    arrays = {
        "ea": ea,
        "dst_t": tr(dst_pad.reshape(TILES, P)),
        "dst_g": dst_pad.reshape(GROUPS // 2, 2 * GE),
        "x": np.asarray(x),
        "wm1": np.asarray(L0_gnn_Wm1), "wm1t": tr(L0_gnn_Wm1), "bm1": np.asarray(L0_gnn_bm1),
        "wm2t": tr(L0_gnn_Wm2), "bm2": np.asarray(L0_gnn_bm2),
        "wm3t": tr(L0_gnn_Wm3), "bm3": np.asarray(L0_gnn_bm3),
        "ln_g": np.asarray(L0_gnn_ln_g), "ln_b": np.asarray(L0_gnn_ln_b),
        "wu1t": tr(L0_gnn_Wu1), "bu1": np.asarray(L0_gnn_bu1),
        "wu2t": tr(L0_gnn_Wu2), "bu2": np.asarray(L0_gnn_bu2),
        "wu3t": tr(L0_gnn_Wu3), "bu3": np.asarray(L0_gnn_bu3),
    }
    nc = bacc.Bacc("TRN2", target_bir_lowering=False, num_devices=1)
    args = [nc.dram_tensor(f"in_{k}", a.shape, mybir.dt.from_np(a.dtype), kind="ExternalInput").ap()
            for k, a in arrays.items()]
    out = nc.dram_tensor("out", (NODES, D), F32, kind="ExternalOutput").ap()
    gnn_kernel(nc, *args, out)
    r = run_bass_kernel_spmd(nc, [{f"in_{k}": a for k, a in arrays.items()}], core_ids=[0])
    return r.results[0]["out"]
```

```python
import concourse.bass as bass
from concourse import mybir
from contextlib import ExitStack
import numpy as np

F32 = mybir.dt.float32
F32R = mybir.dt.float32r
BF16 = mybir.dt.bfloat16
I32 = mybir.dt.int32
ALU = mybir.AluOpType
ACT = mybir.ActivationFunctionType
AX = mybir.AxisListType

NODES, EDGES, D, DE = 6250, 106250, 128, 5
U1, U2 = 214, 172
P = 128
GT = 4
GE = GT * P
PIECE = 8192
PIECES = -(-EDGES // PIECE)
EPAD = PIECES * PIECE
GROUPS = EPAD // GE
TILES = EPAD // P
R = DE + 1
K54 = 9 * R
PC = R * PIECE // P
CHUNK = 2048
CG = CHUNK // GE
PG = PIECE // GE
BODY = PG
TURNS = GROUPS // BODY
W = D + 1
WH = D + 2
WL = WH + D
WIN = 64
NT = -(-NODES // P)
LASTROWS = NODES - (NT - 1) * P
ST = 4
SUPERS = -(-NT // ST)
H1, H2 = U1 // 2, U2 // 2
NB = 7
SLOPE = 0.01
EPS = 1e-5


def gnn_kernel(nc, ea, dst_t, dst_g, x, wm1, wm1t, bm1, wm2t, bm2, wm3t, bm3, ln_g, ln_b,
               wu1t, bu1, wu2t, bu2, wu3t, bu3, out):
    ctx = ExitStack()
    with ctx:
        def sb(name, shape, dt=F32):
            return ctx.enter_context(nc.sbuf_tensor(name, shape, dt))

        def sem(name):
            return ctx.enter_context(nc.semaphore(name))

        parts_dram = nc.dram_tensor("parts_dram", [PIECES, K54, PIECE], BF16)
        wparts_dram = nc.dram_tensor("wparts_dram", [3 * R, 2 * D], BF16)
        meta_dram = nc.dram_tensor("meta_dram", [3, GROUPS], I32)

        ps = ctx.enter_context(nc.psum_tensor("ps", [P, 8, 512], F32))

        ident = sb("ident", [P, P])
        iota = sb("iota", [P, P])
        w1n = sb("w1n", [P, R])
        w1t = sb("w1t", [R, D])
        b2row = sb("b2row", [R, D])
        lin = sb("lin", [R, D])
        wres = sb("wres", [R, 2, D])
        wpart = sb("wpart", [R, 3, 2, D], BF16)
        w54 = sb("w54", [K54, 2, D], BF16)
        w2t = sb("w2t", [D, D])
        w3t = sb("w3t", [D, D])
        bm3b = sb("bm3b", [P, D])
        lng = sb("lng", [P, 2])
        lnb = sb("lnb", [P, 2])
        wu1 = sb("wu1", [P, 2, U1])
        wu2 = sb("wu2", [H1, 2, U2])
        wu3 = sb("wu3", [H2, 2, D])
        bu1c = sb("bu1c", [H1, 2])
        bu2c = sb("bu2c", [H2, 2])
        bu3b = sb("bu3b", [P, D])

        half = sb("half", [P, ST])
        eps = sb("eps", [P, ST])

        ea_sb = sb("ea_sb", [P, PC])
        zero_pc = sb("zero_pc", [P, PC])
        ea_part = sb("ea_part", [P, 3, PC], BF16)

        gmin = sb("gmin", [GROUPS // 2, 2], I32)
        gmax = sb("gmax", [GROUPS // 2, 2], I32)
        gpar = sb("gpar", [GROUPS // 2, 2], I32)
        ghalf = sb("ghalf", [GROUPS // 2, 2], I32)
        gmeta = sb("gmeta", [GROUPS // 2, 3, 2], I32)
        base_b = sb("base_b", [P, GROUPS], I32)
        meta_row = sb("meta_row", [1, 2 * GROUPS], I32)
        span_max = sb("span_max", [1, 1], I32)
        flag = sb("flag", [1, 1], I32)
        dst_sb = sb("dst_sb", [P, TILES], I32)
        dst_rel = sb("dst_rel", [P, TILES])

        a54 = sb("a54", [K54, 2, CHUNK], BF16)
        shared = sb("shared", [P, 4, 2, GE])
        h1, relu2 = (shared[:, n, :, :] for n in range(2))
        h2 = shared[:, 2:4, :, :].rearrange("p a b e -> p (a b) e")
        h2_parts = sb("h2_parts", [P, 4, GT, WL], F32R)
        onehot = sb("onehot", [P, 2, GE], F32R)
        acc = sb("acc", [P, 2, NT, W])

        shift = sb("shift", [P, NT, W])
        x_sb = sb("x_sb", [P, NT, D])
        xb = sb("xb", [P, 2, ST, D])
        agg = sb("agg", [P, 2, ST, W])
        aggT = sb("aggT", [P, ST * P])
        msg = sb("msg", [P, 2, ST, D])
        bn = sb("bn", [P, ST, 12])
        mv = sb("mv", [P, ST, 2])
        rstd = sb("rstd", [P, 2, ST])
        mrs = sb("mrs", [P, 2, ST])
        nrm = sb("nrm", [P, 2, ST, 2 * D])
        nrmT = sb("nrmT", [P, 2, ST * P])
        z1, u1 = (shared[0:H1, n, :, :] for n in range(2))
        z2, u2 = (shared[0:H2, n, :, :] for n in range(2, 4))
        y = sb("y", [P, 2, ST, D])
        ybn = sb("ybn", [P, ST, 6])
        ymv = sb("ymv", [P, ST, 2])
        yrstd = sb("yrstd", [P, 2, ST])
        ymrs = sb("ymrs", [P, 2, ST])
        o_sb = sb("o_sb", [P, 2, ST, D])
        gdst = shift[0:GROUPS // 2, :, :].rearrange("p a b -> p (a b)")[:, 0:2 * GE].bitcast(I32)\
            .rearrange("p (a e) -> p a e", a=2)
        node_iota = shift[:, :, :].rearrange("p a b -> p (a b)")[:, 0:NT * P]

        weights_in = sem("weights_in")
        late_in = sem("late_in")
        b2row_zero = sem("b2row_zero")
        b2row_in = sem("b2row_in")
        x_zero = sem("x_zero")
        ea_in = sem("ea_in")
        dst_in = sem("dst_in")
        consts = sem("consts")
        pool_ident = sem("pool_ident")
        lin_mm = sem("lin_mm")
        wsplit = sem("wsplit")
        w54_in = sem("w54_in")
        split_step = sem("split_step")
        parts_ready = sem("parts_ready")
        parts_out = sem("parts_out")
        wparts_out = sem("wparts_out")
        meta_step = sem("meta_step")
        meta_out = sem("meta_out")
        meta_in = sem("meta_in")
        rel_ready = sem("rel_ready")
        flag_ready = sem("flag_ready")
        ones_ready = sem("ones_ready")
        acc_zero = sem("acc_zero")

        chunk_in = [sem(f"chunk_in{n}") for n in range(2)]
        s1_done = sem("s1_done")
        h1_ready = sem("h1_ready")
        s2_done = sem("s2_done")
        relu2_ready = sem("relu2_ready")
        h2_ready = sem("h2_ready")
        hi_ready = sem("hi_ready")
        lo_ready = sem("lo_ready")
        acc_hi_done = sem("acc_hi_done")
        onehot_ready = sem("onehot_ready")
        s3_done = sem("s3_done")
        acc_done = sem("acc_done")

        g_tile_in = sem("g_tile_in")
        g_iota = sem("g_iota")
        g_s1_done = sem("g_s1_done")
        g_h1_ready = sem("g_h1_ready")
        g_s2_done = sem("g_s2_done")
        g_relu2_ready = sem("g_relu2_ready")
        g_h2_ready = sem("g_h2_ready")
        g_hi_ready = sem("g_hi_ready")
        g_lo_ready = sem("g_lo_ready")
        g_onehot = sem("g_onehot")
        g_s3_done = sem("g_s3_done")
        g_acc_done = sem("g_acc_done")

        edges_done = sem("edges_done")
        shift_in = [sem(f"shift_in{n}") for n in range(2)]
        agg_ready = sem("agg_ready")
        a1_done = sem("a1_done")
        aggT_ready = sem("aggT_ready")
        a2_done = sem("a2_done")
        stats_ready = sem("stats_ready")
        ystats_ready = sem("ystats_ready")
        msg_ready = sem("msg_ready")
        bn_ready = sem("bn_ready")
        rstd_step = sem("rstd_step")
        nrm_ready = sem("nrm_ready")
        xb_ready = sem("xb_ready")
        t_done = sem("t_done")
        nrmT_ready = sem("nrmT_ready")
        u1_done = sem("u1_done")
        z1_ready = sem("z1_ready")
        u1_ready = sem("u1_ready")
        u2_done = sem("u2_done")
        z2_ready = sem("z2_ready")
        u2_ready = sem("u2_ready")
        u3_done = sem("u3_done")
        y_ready = sem("y_ready")
        ybn_ready = sem("ybn_ready")
        yrstd_step = sem("yrstd_step")
        rstd_ready = sem("rstd_ready")
        yrstd_ready = sem("yrstd_ready")
        out_ready = sem("out_ready")
        out_stored = [sem(f"out_stored{n}") for n in range(2)]

        N_WEIGHTS, N_LATE = 5, 14

        def node_steps(eng, step, first, last):
            lo, hi = 3, 9
            for s in range(first, lo):
                step(s, s % 2, lambda q, s=s: 0 <= s + q < SUPERS, s)
            with eng.Fori(0, (hi - lo) // 2) as i:
                for j in range(2):
                    step(2 * i + lo + j, (lo + j) % 2, lambda q: True, None)
            for s in range(hi, last + 1):
                step(s, s % 2, lambda q, s=s: 0 <= s + q < SUPERS, s)

        def tiles_of(s, q, static):
            return ST if static is None or static + q < SUPERS - 1 else NT - ST * (SUPERS - 1)

        def from_tile(s, q):
            return (s + q) * ST

        block = ctx.enter_context(nc.Block())

        @block.sync
        def _(sp):
            sp.dma_start(gdst[:, :, :], dst_g.rearrange("p (a e) -> p a e", a=2)).then_inc(dst_in, 16)
            sp.dma_start(ea_sb[:, :], ea[0]).then_inc(ea_in, 16)
            sp.dma_start(dst_sb[:, :], dst_t).then_inc(dst_in, 16)

            def store_parts(q):
                sp.wait_ge(parts_ready, q + 1)
                for p in range(3):
                    rows = parts_dram[bass.ds(q, 1), 3 * R * p:3 * R * (p + 1), :]
                    sp.dma_start(rows.rearrange("q (rep r) n -> (q rep) (r n)", rep=3)
                                 .rearrange("rep (x c) -> x rep c", x=P),
                                 ea_part[:, p, :].unsqueeze(1).to_broadcast([P, 3, PC])).then_inc(parts_out, 16)

            def load_piece(q):
                sp.dma_start(ea_sb[:, :], ea[bass.ds(q, 1), :, :].rearrange("q p c -> (q p) c")).then_inc(ea_in, 16)

            sp.wait_ge(meta_step, 6)
            sp.dma_start(meta_dram.ap().rearrange("k (p a) -> p k a", a=2), gmeta[:, :, :]).then_inc(meta_out, 16)
            store_parts(0)
            load_piece(1)
            sp.wait_ge(meta_out, 16)
            sp.dma_start(base_b[:, :], meta_dram[0, :].partition_broadcast(P)).then_inc(meta_in, 16)
            sp.dma_start(meta_row[:, :], meta_dram[1:3, :].rearrange("(a k) g -> a (k g)", a=1)).then_inc(meta_in, 16)

            def load_late():
                for dst, src in [
                    (w3t[:, :], wm3t), (bm3b[:, :], bm3.partition_broadcast(P)),
                    (wu1[:, :, :], wu1t.rearrange("(a p) m -> p a m", p=P)),
                    (wu2[:, :, :], wu2t.rearrange("(a p) m -> p a m", p=H1)),
                    (wu3[:, :, :], wu3t.rearrange("(a p) m -> p a m", p=H2)),
                    (bu3b[:, :], bu3.partition_broadcast(P)),
                ]:
                    sp.dma_start(dst, src).then_inc(late_in, 16)
                for dst, src, rows in [(lng, ln_g, P), (lnb, ln_b, P), (bu1c, bu1, H1), (bu2c, bu2, H2)]:
                    sp.dma_start(dst[:, :], src.rearrange("(a p) -> p a", p=rows),
                                 allow_slow_non_contiguous=True).then_inc(late_in, 16)

            def load_x(n):
                a, b = n * (NT // 3), (n + 1) * (NT // 3)
                sp.dma_start(x_sb[:, a:b, :], x[a * P:b * P, :].rearrange("(t p) f -> p t f", p=P)).then_inc(late_in, 16)
                if n == 2:
                    sp.wait_ge(x_zero, 1)
                    sp.dma_start(x_sb[0:LASTROWS, NT - 1, :], x[(NT - 1) * P:NODES, :]).then_inc(late_in, 16)

            def load_chunk(q, k, free):
                if free:
                    sp.wait_ge(s2_done, q * PG + CG * (k - 1))
                sp.dma_start(a54[:, k % 2, :], parts_dram[bass.ds(q, 1), :, k * CHUNK:(k + 1) * CHUNK]
                             .rearrange("q r n -> (q r) n")).then_inc(chunk_in[k % 2], 16)

            sp.wait_ge(parts_out, 48)
            load_chunk(0, 0, False)
            load_chunk(0, 1, False)

            sp.wait_ge(flag_ready, 1)
            general = sp.value_load(flag[0:1, 0:1], min_val=0, max_val=1)
            with sp.If(general < 1):
                def feed(q, first, store, load):
                    if not first:
                        sp.wait_ge(parts_out, 48 * (q + 1))
                        load_chunk(q, 0, True)
                        load_chunk(q, 1, True)
                    load_chunk(q, 2, True)
                    load_chunk(q, 3, True)
                    if store:
                        store_parts(q + 1)
                    if load:
                        load_piece(q + 2)

                feed(0, True, True, True)
                load_late()
                feed(1, False, True, True)
                load_x(0)
                with sp.Fori(2, PIECES - 2) as q:
                    feed(q, False, True, True)
                feed(PIECES - 2, False, True, False)
                load_x(1)
                feed(PIECES - 1, False, False, False)
                load_x(2)
            with sp.Else():
                load_late()
                for n in range(3):
                    load_x(n)
                with sp.Fori(1, PIECES - 1) as q:
                    store_parts(q)
                    load_piece(q + 1)
                store_parts(PIECES - 1)
                sp.wait_ge(parts_out, 48 * PIECES)
                sp.wait_ge(chunk_in[0], 16)
                with sp.Fori(0, PIECES) as q:
                    with sp.Fori(0, PIECE // P) as k:
                        sp.wait_ge(g_s2_done, q * (PIECE // P) + k + 1)
                        sp.dma_start(a54[:, 0, 0:P], parts_dram[bass.ds(q, 1), :, bass.ds(k * P, P)]
                                     .rearrange("q r n -> (q r) n")).then_inc(g_tile_in, 16)

            sp.wait_ge(edges_done, 1)
            for n, (a, b) in enumerate([(0, 2 * ST), (2 * ST, NT)]):
                lo = max(a, 1)
                sp.dma_start(shift[0:WIN, lo:b, :], acc[WIN:P, 1, lo - 1:b - 1, :]).then_inc(shift_in[n], 16)
                sp.dma_start(shift[WIN:P, a:b, :], acc[0:WIN, 1, a:b, :]).then_inc(shift_in[n], 16)

            for s in range(SUPERS):
                t0 = s * ST * P
                sp.wait_ge(out_ready, s + 1)
                if s < SUPERS - 1:
                    sp.dma_start(out[t0:t0 + ST * P, :].rearrange("(t p) f -> p t f", p=P), o_sb[:, s % 2, :, :])\
                        .then_inc(out_stored[s % 2], 16)
                else:
                    sp.dma_start(out[t0:NODES, :], o_sb[0:LASTROWS, s % 2, 0, :]).then_inc(out_stored[s % 2], 16)
            sp.wait_ge(out_stored[0], 16 * ((SUPERS + 1) // 2))
            sp.wait_ge(out_stored[1], 16 * (SUPERS // 2))

        @block.scalar
        def _(act):
            act.dma_start(w1n[:, 0:DE], wm1).then_inc(weights_in, 16)
            act.dma_start(w1n[:, DE:R], bm1.rearrange("(p a) -> p a", a=1)).then_inc(weights_in, 16)
            act.dma_start(w1t[0:DE, :], wm1t).then_inc(weights_in, 16)
            act.dma_start(w1t[DE:R, :], bm1.rearrange("(a p) -> a p", a=1)).then_inc(weights_in, 16)
            act.dma_start(w2t[:, :], wm2t).then_inc(weights_in, 16)
            act.wait_ge(b2row_zero, 1)
            act.dma_start(b2row[DE:R, :], bm2.rearrange("(a p) -> a p", a=1)).then_inc(b2row_in, 16)

            act.wait_ge(wsplit, 6)
            act.dma_start(wparts_dram.ap().rearrange("(k r) n -> r k n", r=R),
                          wpart[:, :, :, :].rearrange("r k h n -> r k (h n)")).then_inc(wparts_out, 16)
            act.wait_ge(wparts_out, 16)
            act.dma_start(w54[:, :, :].rearrange("k h n -> k (h n)"),
                          wparts_dram.ap().partition_broadcast(3)).then_inc(w54_in, 16)

            act.wait_ge(flag_ready, 1)
            general = act.value_load(flag[0:1, 0:1], min_val=0, max_val=1)
            with act.If(general < 1):
                def first_relu(g, j):
                    act.wait_ge(s1_done, g + 1)
                    act.activation(h1[:, j % 2, :], ps[:, j % 2, :], ACT.Relu, scale=1.0 - SLOPE).then_inc(h1_ready, 1)

                def second_relu(g, j):
                    act.wait_ge(s2_done, g + 1)
                    act.activation(relu2[:, j % 2, :], ps[:, 2 + j % 2, :], ACT.Relu, scale=1.0 - SLOPE)\
                        .then_inc(relu2_ready, 1)

                def high_part(g, j):
                    act.wait_ge(h2_ready, g + 1)
                    act.activation(h2_parts[:, j % 4, :, 0:D], h2[:, j % 4, :].rearrange("p (t f) -> p t f", t=GT),
                                   ACT.Copy).then_inc(hi_ready, 1)

                def act_edge_step(s, j, peeled, last=False):
                    if not peeled:
                        for value in (s - 1, s - 2, s + 1):
                            act.compute_val(value)
                    if not (peeled and s < 2) and not (last and s - 2 >= GROUPS):
                        second_relu(s - 2, (j - 2) % BODY)
                    if not (peeled and s < 3):
                        high_part(s - 3, (j - 3) % BODY)
                    if not last:
                        first_relu(s, j)

                for j in range(BODY):
                    act_edge_step(j, j, True)
                with act.Fori(1, TURNS) as i:
                    for j in range(BODY):
                        act_edge_step(i * BODY + j, j, False)
                for j in range(3):
                    act_edge_step(GROUPS + j, j, True, True)
            with act.Else():
                with act.Fori(0, TILES) as t:
                    act.wait_ge(g_s1_done, t + 1)
                    act.activation(h1[:, 0, 0:P], ps[:, 0, 0:P], ACT.Relu, scale=1.0 - SLOPE).then_inc(g_h1_ready, 1)
                    act.wait_ge(g_s2_done, t + 2)
                    act.activation(relu2[:, 0, 0:P], ps[:, 1, 0:P], ACT.Relu, scale=1.0 - SLOPE).then_inc(g_relu2_ready, 1)
                    act.wait_ge(g_h2_ready, t + 1)
                    act.activation(h2_parts[:, 0, 0, 0:D], h2[:, 0, 0:P], ACT.Copy).then_inc(g_hi_ready, 1)

            act.wait_ge(late_in, 16 * N_LATE)

            def copy_aggT(s, q, static):
                nt = tiles_of(s, q, static)
                act.wait_ge(a1_done, s + q + 1)
                if static is None or static + q >= 1:
                    act.wait_ge(a2_done, s + q)
                act.activation(aggT[:, 0:nt * P], ps[:, 0, 0:nt * P], ACT.Copy).then_inc(aggT_ready, 1)

            def scale_nrmT(s, static):
                n = tiles_of(s, 0, static) * P
                if static is None or static >= 1:
                    act.wait_ge(u1_done, 2 * s)
                for h in range(2):
                    act.wait_ge(t_done, 2 * s + h + 1)
                    act.activation(nrmT[:, h, 0:n], ps[:, 1 + h, 0:n], ACT.Identity,
                                   bias=lnb[:, h:h + 1], scale=lng[:, h:h + 1]).then_inc(nrmT_ready, 1)

            def add_bias(s, static, done, read, z, bank, bias, rows, ready):
                n = tiles_of(s, 0, static) * P
                for h in range(2):
                    act.wait_ge(done, 2 * s + h + 1)
                    if static is None or static >= 1:
                        act.wait_ge(read, 2 * s + h - 1)
                    act.activation(z[:, h, 0:n], ps[0:rows, bank + h, 0:n], ACT.Identity, bias=bias[:, h:h + 1])\
                        .then_inc(ready, 1)

            def normalise(s, q, par, static, first):
                nt = tiles_of(s, q, static)
                t0 = from_tile(s, q)
                b = (par + q) % 2

                def scaled(src, t, half_):
                    return act.activation(nrm[:, b, t, half_ * D:(half_ + 1) * D], src, ACT.Identity,
                                          bias=mrs[:, b, t:t + 1], scale=rstd[:, b, t:t + 1])

                if first:
                    act.wait_ge(rstd_ready, s + q + 1)
                    if static is None or static + q >= 2:
                        act.wait_ge(t_done, 2 * (s + q - 1))
                    if static != -1:
                        for t in range(nt):
                            last = scaled(x_sb[:, bass.ds(t0 + t, 1), :].rearrange("p a f -> p (a f)"), t, 0)
                        last.then_inc(nrm_ready, 1)
                for t in range(nt // 2) if first else range(nt // 2, nt):
                    last = scaled(msg[:, b, t, :], t, 1)
                if not first:
                    last.then_inc(nrm_ready, 1)

            def finish(s, q, par, static):
                nt = tiles_of(s, q, static)
                b = 1 - par
                act.wait_ge(yrstd_ready, s + q + 1)
                if static is None:
                    act.wait_ge(out_stored[b], (s + q - b) * 8)
                elif static + q >= 2:
                    act.wait_ge(out_stored[b], 16 * ((static + q - b) // 2))
                for t in range(nt):
                    last = act.activation(o_sb[:, b, t, :], y[:, b, t, :], ACT.Identity,
                                          bias=ymrs[:, b, t:t + 1], scale=yrstd[:, b, t:t + 1])
                last.then_inc(out_ready, 1)

            def act_step(s, par, has, static):
                if has(0):
                    scale_nrmT(s, static)
                if has(2):
                    copy_aggT(s, 2, static)
                if has(1):
                    normalise(s, 1, par, static, True)
                if has(0):
                    add_bias(s, static, u1_done, u1_ready, z1, 3, bu1c, H1, z1_ready)
                hurry = static == SUPERS - 1
                if has(-1) and not hurry:
                    finish(s, -1, par, static)
                if has(1):
                    normalise(s, 1, par, static, False)
                if has(0):
                    add_bias(s, static, u2_done, u2_ready, z2, 5, bu2c, H2, z2_ready)
                if hurry:
                    finish(s, -1, par, static)

            node_steps(act, act_step, -2, SUPERS)

        @block.gpsimd
        def _(pool):
            pool.memset(b2row[:, :], 0.0).then_inc(b2row_zero, 1)
            pool.iota(iota[:, :], pattern=[[1, P]], base=0, channel_multiplier=0,
                      allow_small_or_imprecise_dtypes=True).then_inc(consts, 1)
            pool.memset(zero_pc[:, :], 0.0).then_inc(split_step, 1)

            def split_quarter(q, n, first):
                pool.wait_ge(split_step, 3 * q + n + 1)
                if n == 0:
                    pool.wait_ge(ea_in, 16 * (q + 1))
                    if not first:
                        pool.wait_ge(parts_out, 48 * q)
                    pool.tensor_tensor(ea_part[:, 0, :], ea_sb[:, :], zero_pc[:, :], ALU.add).then_inc(split_step, 1)
                elif n == 1:
                    pool.tensor_tensor(ea_sb[:, :], ea_sb[:, :], ea_part[:, 0, :], ALU.subtract).then_inc(split_step, 1)
                elif n == 2:
                    pool.tensor_tensor(ea_part[:, 1, :], ea_sb[:, :], zero_pc[:, :], ALU.add).then_inc(split_step, 1)
                else:
                    pool.tensor_tensor(ea_part[:, 2, :], ea_sb[:, :], ea_part[:, 1, :], ALU.subtract).then_inc(parts_ready, 1)

            def split_piece(q, first):
                for n in range(4):
                    split_quarter(q, n, first)

            split_piece(0, True)
            pool.memset(h2_parts[:, :, :, D:D + 1].bitcast(F32), 1.0).then_inc(ones_ready, 1)
            pool.memset(h2_parts[:, :, :, D + 1:WH].bitcast(F32), 0.0).then_inc(ones_ready, 1)
            pool.memset(x_sb[:, NT - 1, :], 0.0).then_inc(x_zero, 1)
            pool.memset(ident[:, :], 0.0).then_inc(pool_ident, 1)
            pool.wait_ge(pool_ident, 1)
            pool.affine_select(out=ident[:, :], in_=ident[:, :], compare_op=ALU.not_equal, fill=1.0,
                               base=0, pattern=[[-1, P]], channel_multiplier=1).then_inc(pool_ident, 1)

            pool.memset(half[:, :], -0.5).then_inc(consts, 1)
            pool.memset(eps[:, :], EPS).then_inc(consts, 1)
            pool.memset(acc[:, 1, :, :], 0.0).then_inc(acc_zero, 1)
            pool.memset(acc[:, 0, NT // 2:NT, :], 0.0).then_inc(acc_zero, 1)

            pool.wait_ge(flag_ready, 1)
            general = pool.value_load(flag[0:1, 0:1], min_val=0, max_val=1)

            with pool.If(general < 1):
                def low_part(g, j):
                    pool.wait_ge(hi_ready, g + 1)
                    pool.tensor_tensor(h2_parts[:, j % 4, :, WH:WL], h2[:, j % 4, :].rearrange("p (t f) -> p t f", t=GT),
                                       h2_parts[:, j % 4, :, 0:D].bitcast(F32), ALU.subtract).then_inc(lo_ready, 1)

                def piece_turn(q, split):
                    for j in range(PG):
                        if split and j % 2 == 0 and j < 8:
                            split_quarter(q + 1, j // 2, False)
                        low_part(q * PG + j, j)

                piece_turn(0, True)
                with pool.Fori(1, PIECES - 1) as q:
                    piece_turn(q, True)
                piece_turn(PIECES - 1, False)
            with pool.Else():
                pool.iota(node_iota, pattern=[[1, NT * P]], base=0, channel_multiplier=0,
                          allow_small_or_imprecise_dtypes=True).then_inc(g_iota, 1)
                with pool.Fori(1, PIECES) as q:
                    split_piece(q, False)
                with pool.Fori(0, TILES) as t:
                    pool.wait_ge(g_hi_ready, t + 1)
                    pool.tensor_tensor(h2_parts[:, 0, 0, WH:WL], h2[:, 0, 0:P], h2_parts[:, 0, 0, 0:D].bitcast(F32),
                                       ALU.subtract).then_inc(g_lo_ready, 1)

            pool.wait_ge(late_in, 16 * N_LATE)
            pool.wait_ge(consts, 3)

            def add_bu3(s, par, static):
                nt = tiles_of(s, 0, static)
                if static is None or static >= 2:
                    pool.wait_ge(y_ready, s - 1)
                pool.tensor_tensor(xb[:, par, 0:nt, :], x_sb[:, bass.ds(from_tile(s, 0), nt), :],
                                   bu3b[:, :].unsqueeze(1).to_broadcast([P, nt, D]), ALU.add).then_inc(xb_ready, 1)

            def scales(n, nt, b, ready, step, used, used_per, used_from, mv_, r, m, done):
                pool.wait_ge(ready, n + 1)
                if used_from:
                    pool.wait_ge(used, (n - 1) * used_per)
                pool.tensor_tensor(r[:, b, 0:nt], mv_[:, 0:nt, 1], eps[:, 0:nt], ALU.add).then_inc(step, 1)
                pool.tensor_scalar(m[:, b, 0:nt], mv_[:, 0:nt, 0], -1.0, None, ALU.mult).then_inc(step, 1)
                pool.wait_ge(step, 3 * n + 2)
                pool.tensor_tensor(r[:, b, 0:nt], r[:, b, 0:nt], half[:, 0:nt], ALU.pow).then_inc(step, 1)
                pool.wait_ge(step, 3 * n + 3)
                pool.tensor_tensor(m[:, b, 0:nt], m[:, b, 0:nt], r[:, b, 0:nt], ALU.mult).then_inc(done, 1)

            def pool_step(s, par, has, static):
                if has(-1):
                    scales(s - 1, tiles_of(s, -1, static), 1 - par, ystats_ready, yrstd_step, out_ready, 1,
                           static is None or static >= 3, ymv, yrstd, ymrs, yrstd_ready)
                if has(2):
                    scales(s + 2, tiles_of(s, 2, static), par, stats_ready, rstd_step, nrm_ready, 2,
                           static is None or static >= 0, mv, rstd, mrs, rstd_ready)
                if has(0):
                    add_bu3(s, par, static)

            node_steps(pool, pool_step, -2, SUPERS)

        @block.vector
        def _(dve):
            dve.wait_ge(dst_in, 32)
            dve.tensor_reduce(gmin[:, :], gdst[:, :, :], AX.X, ALU.min).then_inc(meta_step, 1)
            dve.tensor_reduce(gmax[:, :], gdst[:, :, :], AX.X, ALU.max).then_inc(meta_step, 1)
            dve.wait_ge(meta_step, 2)
            dve.tensor_scalar(gmeta[:, 0, :], gmin[:, :], -WIN, None, ALU.bitwise_and).then_inc(meta_step, 1)
            dve.tensor_scalar(gpar[:, :], gmin[:, :], 6, 1, ALU.logical_shift_right, ALU.bitwise_and)
            dve.tensor_scalar(ghalf[:, :], gmin[:, :], 7, None, ALU.logical_shift_right).then_inc(meta_step, 1)
            dve.wait_ge(meta_step, 4)
            dve.tensor_tensor(gmeta[:, 2, :], gmax[:, :], gmeta[:, 0, :], ALU.subtract).then_inc(meta_step, 1)
            dve.scalar_tensor_tensor(out=gmeta[:, 1, :], in0=gpar[:, :], scalar=float(NT), in1=ghalf[:, :],
                                     op0=ALU.mult, op1=ALU.add).then_inc(meta_step, 1)

            dve.wait_ge(lin_mm, 1)
            dve.wait_ge(b2row_in, 16)
            dve.scalar_tensor_tensor(out=wres[:, 1, :], in0=ps[0:R, 7, 0:D], scalar=SLOPE, in1=b2row[:, :],
                                     op0=ALU.mult, op1=ALU.add)
            dve.tensor_copy(wres[:, 0, :], w1t[:, :]).then_inc(wsplit, 1)
            dve.wait_ge(wsplit, 1)
            for part in range(3):
                dve.tensor_copy(wpart[:, part, :, :], wres[:, :, :]).then_inc(wsplit, 1)
                if part < 2:
                    dve.wait_ge(wsplit, 2 + 2 * part)
                    dve.tensor_tensor(wres[:, :, :], wres[:, :, :], wpart[:, part, :, :], ALU.subtract).then_inc(wsplit, 1)
                    dve.wait_ge(wsplit, 3 + 2 * part)

            dve.memset(acc[:, 0, 0:NT // 2, :], 0.0).then_inc(acc_zero, 1)
            dve.wait_ge(meta_in, 32)
            dve.tensor_reduce(span_max[:, :], meta_row[:, GROUPS:2 * GROUPS], AX.X, ALU.max).then_inc(meta_step, 1)
            dve.wait_ge(meta_step, 7)
            dve.tensor_scalar(flag[:, :], span_max[:, :], float(P), None, ALU.is_ge).then_inc(flag_ready, 1)
            dve.tensor_tensor(dst_rel[:, :].rearrange("p (g t) -> p g t", t=GT),
                              dst_sb[:, :].rearrange("p (g t) -> p g t", t=GT),
                              base_b[:, :].unsqueeze(2).to_broadcast([P, GROUPS, GT]),
                              ALU.subtract).then_inc(rel_ready, 1)

            dve.wait_ge(acc_zero, 3)
            dve.wait_ge(rel_ready, 1)
            dve.wait_ge(consts, 1)
            dve.wait_ge(flag_ready, 1)
            general = dve.value_load(flag[0:1, 0:1], min_val=0, max_val=1)

            def leaky(out_, in_):
                return dve.scalar_tensor_tensor(out=out_, in0=in_, scalar=SLOPE, in1=in_, op0=ALU.mult, op1=ALU.max)

            def leaky_sum(out_, z, relu):
                return dve.scalar_tensor_tensor(out=out_, in0=z, scalar=SLOPE, in1=relu, op0=ALU.mult, op1=ALU.add)

            with dve.If(general < 1):
                def second_leaky(g, j):
                    dve.wait_ge(relu2_ready, g + 1)
                    leaky_sum(h2[:, j % 4, :], ps[:, 2 + j % 2, :], relu2[:, j % 2, :]).then_inc(h2_ready, 1)

                def make_onehot(g, j):
                    dve.tensor_tensor(onehot[:, j % 2, :].rearrange("p (t n) -> p t n", n=P),
                                      iota[:, :].unsqueeze(1).to_broadcast([P, GT, P]),
                                      dst_rel[:, bass.ds(g * GT, GT)].unsqueeze(2).to_broadcast([P, GT, P]),
                                      ALU.is_equal).then_inc(onehot_ready, 1)

                def window(g):
                    slot = dve.value_load(meta_row[0:1, bass.ds(g, 1)], min_val=0, max_val=2 * NT - 1)
                    return acc[:, :, :, :].rearrange("p a b c -> p (a b) c")[:, bass.ds(slot, 1), :]\
                        .rearrange("p a c -> p (a c)")

                def add_high(g, j, peeled, dst):
                    if not (peeled and g < 1):
                        dve.wait_ge(acc_done, g)
                    dve.tensor_tensor(dst, ps[:, 4 + j % 4, 0:W], dst, ALU.add).then_inc(acc_hi_done, 1)

                def add_low(g, j, dst):
                    dve.wait_ge(acc_hi_done, g + 1)
                    dst = dst[:, 0:D]
                    dve.tensor_tensor(dst, ps[:, 4 + j % 4, WH:WL], dst, ALU.add).then_inc(acc_done, 1)

                LAG = 5

                def dve_edge_step(s, j, peeled, last=False):
                    if not peeled:
                        for value in (s - LAG, s - LAG + 1, s):
                            dve.compute_val(value)
                    adds = not (peeled and s < LAG)
                    if adds:
                        dst = window(s - LAG)
                        dve.wait_ge(s3_done, s - LAG + 1)
                    if not (peeled and s < 3) and not (last and s - 3 >= GROUPS):
                        make_onehot(s - 3, (j - 3) % BODY)
                    if adds:
                        add_high(s - LAG, (j - LAG) % BODY, peeled, dst)
                    if not (peeled and s < 1) and not (last and s - 1 >= GROUPS):
                        second_leaky(s - 1, (j - 1) % BODY)
                    if adds:
                        add_low(s - LAG, (j - LAG) % BODY, dst)

                for j in range(BODY):
                    dve_edge_step(j, j, True)
                with dve.Fori(1, TURNS) as i:
                    for j in range(BODY):
                        dve_edge_step(i * BODY + j, j, False)
                for j in range(LAG):
                    dve_edge_step(GROUPS + j, j, True, True)
                dve.wait_ge(acc_done, GROUPS)
            with dve.Else():
                dve.wait_ge(g_iota, 1)
                with dve.Fori(0, TILES) as t:
                    dve.wait_ge(g_relu2_ready, t + 1)
                    leaky_sum(h2[:, 0, 0:P], ps[:, 1, 0:P], relu2[:, 0, 0:P]).then_inc(g_h2_ready, 1)
                    for w in range(NB):
                        n = t * NB + w
                        dve.tensor_scalar(onehot[:, :, :].rearrange("p a b -> p (a b)")[:, 0:NB * P],
                                          node_iota[:, w * NB * P:(w + 1) * NB * P],
                                          dst_sb[:, bass.ds(t, 1)], None, ALU.is_equal).then_inc(g_onehot, 1)
                        dve.wait_ge(g_s3_done, n + 1)
                        for bank, (a, b) in enumerate([(0, 3), (3, 6), (6, NB)]):
                            dst = acc[:, 0, w * NB + a:w * NB + b, :]
                            last = dve.tensor_tensor(
                                dst, ps[:, 2 + bank, 0:(b - a) * WH].rearrange("p (a c) -> p a c", c=WH)[:, :, 0:W],
                                dst, ALU.add)
                        last.then_inc(g_acc_done, 1)
                        dve.wait_ge(g_acc_done, n + 1)
            dve.memset(shift[0:WIN, 0, :], 0.0).then_inc(edges_done, 1)
            dve.wait_ge(late_in, 16 * N_LATE)
            dve.wait_ge(edges_done, 1)

            def gather(s, q, par, static):
                nt = tiles_of(s, q, static)
                t0 = from_tile(s, q)
                b = 1 - par
                if static is not None and static + q in (0, 2):
                    dve.wait_ge(shift_in[(static + q) // 2], 32)
                if static is None or static + q >= 2:
                    dve.wait_ge(a1_done, s + q - 1)
                dve.tensor_tensor(agg[:, b, 0:nt, :], acc[:, 0, bass.ds(t0, nt), :], shift[:, bass.ds(t0, nt), :],
                                  ALU.add).then_inc(agg_ready, 1)

            def x_stats(s, q, static):
                nt = tiles_of(s, q, static)
                t0 = from_tile(s, q)
                if static is None or static + q >= 1:
                    dve.wait_ge(stats_ready, s + q)
                for t in range(nt):
                    dve.bn_stats(bn[:, t, 0:6], x_sb[:, bass.ds(t0 + t, 1), :].rearrange("p a f -> p (a f)"))

            def messages(s, q, par, static):
                nt = tiles_of(s, q, static)
                b = par
                dve.wait_ge(a2_done, s + q + 1)
                dve.wait_ge(agg_ready, s + q + 1)
                if static is None or static + q >= 2:
                    dve.wait_ge(nrm_ready, 2 * (s + q - 1))
                if static is None or static + q >= 1:
                    dve.wait_ge(rstd_ready, s + q)
                for t in range(nt):
                    last = dve.scalar_tensor_tensor(out=msg[:, b, t, :], in0=bm3b[:, :], scalar=agg[:, b, t, D:W],
                                                    in1=ps[:, 0, t * P:(t + 1) * P], op0=ALU.mult, op1=ALU.add)
                last.then_inc(msg_ready, 1)
                dve.wait_ge(msg_ready, s + q + 1)
                for t in range(nt):
                    last = dve.bn_stats(bn[:, t, 6:12], msg[:, b, t, :])
                last.then_inc(bn_ready, 1)

            def moments(s, q, par, static):
                nt = tiles_of(s, q, static)
                for t in range(nt):
                    last = dve.bn_aggr(mv[:, t, :], bn[:, t, :])
                last.then_inc(stats_ready, 1)

            def mlp_leaky(s, static, z_ready, read, read_per, u, z, ready):
                n = tiles_of(s, 0, static) * P
                for h in range(2):
                    if h == 0 and (static is None or static >= 1):
                        dve.wait_ge(read, read_per * s)
                    dve.wait_ge(z_ready, 2 * s + h + 1)
                    leaky(u[:, h, 0:n], z[:, h, 0:n]).then_inc(ready, 1)

            def residual(s, q, par, static):
                nt = tiles_of(s, q, static)
                b = 1 - par
                dve.wait_ge(u3_done, s + q + 1)
                dve.wait_ge(xb_ready, s + q + 1)
                if static is None or static + q >= 2:
                    dve.wait_ge(out_ready, s + q - 1)
                dve.tensor_tensor(y[:, b, 0:nt, :], ps[:, 7, 0:nt * P].rearrange("p (t f) -> p t f", f=D),
                                  xb[:, b, 0:nt, :], ALU.add).then_inc(y_ready, 1)
                if static is None or static + q >= 1:
                    dve.wait_ge(yrstd_ready, s + q)
                dve.wait_ge(y_ready, s + q + 1)
                for t in range(nt):
                    last = dve.bn_stats(ybn[:, t, :], y[:, b, t, :])
                last.then_inc(ybn_ready, 1)


            def y_moments(s, q, par, static):
                nt = tiles_of(s, q, static)
                for t in range(nt):
                    last = dve.bn_aggr(ymv[:, t, :], ybn[:, t, :])
                last.then_inc(ystats_ready, 1)

            def normalise_first():
                dve.wait_ge(rstd_ready, 1)
                for t in range(ST):
                    last = dve.tensor_scalar(nrm[:, 0, t, 0:D], x_sb[:, t, :], rstd[:, 0, t:t + 1], mrs[:, 0, t:t + 1],
                                             ALU.mult, ALU.add)
                last.then_inc(nrm_ready, 1)

            def dve_step(s, par, has, static):
                if has(-1):
                    residual(s, -1, par, static)
                    dve.wait_ge(ybn_ready, s)
                if has(2) and static != -2:
                    x_stats(s, 2, static)
                if has(-1):
                    y_moments(s, -1, par, static)
                if has(0):
                    mlp_leaky(s, static, z1_ready, u2_done, 2, u1, z1, u1_ready)
                if static == -3:
                    x_stats(0, 0, 0)
                if static == -2:
                    gather(s, 3, par, static)
                if static == -1:
                    normalise_first()
                if has(2):
                    messages(s, 2, par, static)
                    dve.wait_ge(bn_ready, s + 3)
                if has(3) and static != -2:
                    gather(s, 3, par, static)
                if has(2):
                    moments(s, 2, par, static)
                if has(0):
                    mlp_leaky(s, static, z2_ready, u3_done, 1, u2, z2, u2_ready)

            node_steps(dve, dve_step, -3, SUPERS)

        @block.tensor
        def _(pe):
            pe.wait_ge(weights_in, 16 * N_WEIGHTS)
            pe.matmul(ps[0:R, 7, 0:D], w1n[:, :], w2t[:, :], start=True, stop=True).then_inc(lin_mm, 1)
            pe.wait_ge(w54_in, 16)
            pe.wait_ge(flag_ready, 1)
            general = pe.value_load(flag[0:1, 0:1], min_val=0, max_val=1)
            with pe.If(general < 1):
                def layer1(g, j, turn):
                    if j % CG == 0:
                        n = j // CG
                        pe.wait_ge(chunk_in[n % 2], turn * (8 * BODY // CG) + 16 * (n // 2 + 1))
                    e0 = (j % CG) * GE
                    pe.matmul(ps[:, j % 2, :], w54[:, 0, :], a54[:, j // CG % 2, e0:e0 + GE],
                              start=True, stop=True).then_inc(s1_done, 1)

                def layer2(g, j, peeled):
                    if not (peeled and g < 2):
                        pe.wait_ge(h2_ready, g - 1)
                    pe.wait_ge(h1_ready, g + 1)
                    for t in range(GT):
                        pe.matmul(ps[:, 2 + j % 2, t * P:(t + 1) * P], h1[:, j % 2, t * P:(t + 1) * P],
                                  w2t[:, :], start=t == 0, stop=False, skip_group_check=True)
                    for t in range(GT):
                        e0 = (j % CG) * GE + t * P
                        last = pe.matmul(ps[:, 2 + j % 2, t * P:(t + 1) * P], a54[:, j // CG % 2, e0:e0 + P],
                                         w54[:, 1, :], start=False, stop=True, skip_group_check=True)
                    last.then_inc(s2_done, 1)

                def edge_sum(g, j):
                    pe.wait_ge(lo_ready, g + 1)
                    pe.wait_ge(onehot_ready, g + 1)
                    for t in range(GT):
                        last = pe.matmul(ps[:, 4 + j % 4, 0:WL], onehot[:, j % 2, t * P:(t + 1) * P],
                                         h2_parts[:, j % 4, t, :], start=t == 0, stop=t == GT - 1)
                    last.then_inc(s3_done, 1)

                LAG = 5

                def pe_edge_step(s, j, turn, peeled, last=False):
                    if not peeled:
                        for value in (s - 1, s - 3, s - 4):
                            pe.compute_val(value)
                    if not (peeled and s < 2) and not (last and s - 2 >= GROUPS):
                        layer2(s - 2, (j - 2) % BODY, peeled)
                    if not last:
                        layer1(s, j, turn)
                    if not (peeled and s < LAG):
                        edge_sum(s - LAG, (j - LAG) % BODY)

                pe.wait_ge(ones_ready, 2)
                for j in range(BODY):
                    pe_edge_step(j, j, 0, True)
                with pe.Fori(1, TURNS) as i:
                    for j in range(BODY):
                        pe_edge_step(i * BODY + j, j, i, False)
                for j in range(LAG):
                    pe_edge_step(GROUPS + j, j, None, True, True)
            with pe.Else():
                pe.wait_ge(ones_ready, 2)
                pe.sem_inc(g_s2_done, 1)
                with pe.Fori(0, TILES) as t:
                    pe.wait_ge(g_tile_in, 16 * (t + 1))
                    pe.matmul(ps[:, 0, 0:P], w54[:, 0, :], a54[:, 0, 0:P], start=True, stop=True).then_inc(g_s1_done, 1)
                    pe.wait_ge(g_h1_ready, t + 1)
                    pe.matmul(ps[:, 1, 0:P], a54[:, 0, 0:P], w54[:, 1, :], start=True, stop=False)
                    pe.matmul(ps[:, 1, 0:P], h1[:, 0, 0:P], w2t[:, :], start=False, stop=True).then_inc(g_s2_done, 1)
                    pe.wait_ge(g_lo_ready, t + 1)
                    for w in range(NB):
                        pe.wait_ge(g_onehot, t * NB + w + 1)
                        for k in range(NB):
                            c0 = (k % 3) * WH
                            hot = onehot[:, k * P // GE, k * P % GE:k * P % GE + P]
                            pe.matmul(ps[:, 2 + k // 3, c0:c0 + WH], hot, h2_parts[:, 0, 0, 0:WH], start=True, stop=False)
                            last = pe.matmul(ps[:, 2 + k // 3, c0:c0 + D], hot, h2_parts[:, 0, 0, WH:WL],
                                             start=False, stop=True)
                        last.then_inc(g_s3_done, 1)

            pe.wait_ge(pool_ident, 2)
            pe.wait_ge(late_in, 16 * N_LATE)

            def transpose_agg(s, q, par, static):
                nt = tiles_of(s, q, static)
                pe.wait_ge(agg_ready, s + q + 1)
                if static is None or static + q >= 1:
                    pe.wait_ge(msg_ready, s + q)
                for t in range(nt):
                    last = pe.transpose(ps[:, 0, t * P:(t + 1) * P], agg[:, par, t, 0:D], ident[:, :])
                last.then_inc(a1_done, 1)

            def product_msg(s, q, static):
                nt = tiles_of(s, q, static)
                pe.wait_ge(aggT_ready, s + q + 1)
                for t in range(nt):
                    last = pe.matmul(ps[:, 0, t * P:(t + 1) * P], aggT[:, t * P:(t + 1) * P], w3t[:, :],
                                     start=True, stop=True)
                last.then_inc(a2_done, 1)

            def transpose_nrm(s, par, static):
                nt = tiles_of(s, 0, static)
                pe.wait_ge(nrm_ready, 2 * (s + 1))
                if static is None or static >= 1:
                    pe.wait_ge(nrmT_ready, 2 * s)
                for h in range(2):
                    for t in range(nt):
                        last = pe.transpose(ps[:, 1 + h, t * P:(t + 1) * P], nrm[:, par, t, h * D:(h + 1) * D], ident[:, :])
                    last.then_inc(t_done, 1)

            def mlp_layer(s, static, in_ready, read, bank, w, act_in, rows, done):
                n = tiles_of(s, 0, static) * P
                if static is None or static >= 1:
                    pe.wait_ge(read, 2 * s)
                for k in range(2):
                    pe.wait_ge(in_ready, 2 * s + k + 1)
                    for m in range(2):
                        last = pe.matmul(ps[0:rows, bank + m, 0:n], w[:, k, m * rows:(m + 1) * rows],
                                         act_in[:, k, 0:n], start=k == 0, stop=k == 1)
                        if k == 1:
                            last.then_inc(done, 1)

            def last_layer(s, q, static):
                nt = tiles_of(s, q, static)
                if static is None or static + q >= 1:
                    pe.wait_ge(y_ready, s + q)
                for k in range(2):
                    pe.wait_ge(u2_ready, 2 * (s + q) + k + 1)
                    for t in range(nt):
                        last = pe.matmul(ps[:, 7, t * P:(t + 1) * P], u2[:, k, t * P:(t + 1) * P], wu3[:, k, :],
                                         start=k == 0 and t == 0, stop=k == 1, skip_group_check=True)
                last.then_inc(u3_done, 1)

            def pe_step(s, par, has, static):
                if has(0):
                    transpose_nrm(s, par, static)
                if has(-1):
                    last_layer(s, -1, static)
                if has(2):
                    transpose_agg(s, 2, par, static)
                if has(0):
                    mlp_layer(s, static, nrmT_ready, z1_ready, 3, wu1, nrmT, H1, u1_done)
                if has(2):
                    product_msg(s, 2, static)
                if has(0):
                    mlp_layer(s, static, u1_ready, z2_ready, 5, wu2, u1, H2, u2_done)

            node_steps(pe, pe_step, -2, SUPERS)


def kernel(x, src, dst, edge_attr_5, L0_gnn_Wm1, L0_gnn_bm1, L0_gnn_Wm2, L0_gnn_bm2, L0_gnn_Wm3, L0_gnn_bm3,
           L0_gnn_ln_g, L0_gnn_ln_b, L0_gnn_Wu1, L0_gnn_bu1, L0_gnn_Wu2, L0_gnn_bu2, L0_gnn_Wu3, L0_gnn_bu3):
    import concourse.bacc as bacc
    from concourse.bass_utils import run_bass_kernel_spmd

    ea = np.zeros((R, EPAD), np.float32)
    ea[DE] = 1.0
    ea[:DE, :EDGES] = np.asarray(edge_attr_5).T
    ea = np.ascontiguousarray(ea.reshape(R, PIECES, PIECE).transpose(1, 0, 2)).reshape(PIECES, P, PC)
    dst_pad = np.full(EPAD, NODES, np.int32)
    dst_pad[:EDGES] = np.asarray(dst)

    def tr(w):
        return np.ascontiguousarray(np.asarray(w).T)

    arrays = {
        "ea": ea,
        "dst_t": tr(dst_pad.reshape(TILES, P)),
        "dst_g": dst_pad.reshape(GROUPS // 2, 2 * GE),
        "x": np.asarray(x),
        "wm1": np.asarray(L0_gnn_Wm1), "wm1t": tr(L0_gnn_Wm1), "bm1": np.asarray(L0_gnn_bm1),
        "wm2t": tr(L0_gnn_Wm2), "bm2": np.asarray(L0_gnn_bm2),
        "wm3t": tr(L0_gnn_Wm3), "bm3": np.asarray(L0_gnn_bm3),
        "ln_g": np.asarray(L0_gnn_ln_g), "ln_b": np.asarray(L0_gnn_ln_b),
        "wu1t": tr(L0_gnn_Wu1), "bu1": np.asarray(L0_gnn_bu1),
        "wu2t": tr(L0_gnn_Wu2), "bu2": np.asarray(L0_gnn_bu2),
        "wu3t": tr(L0_gnn_Wu3), "bu3": np.asarray(L0_gnn_bu3),
    }
    nc = bacc.Bacc("TRN2", target_bir_lowering=False, num_devices=1)
    args = [nc.dram_tensor(f"in_{k}", a.shape, mybir.dt.from_np(a.dtype), kind="ExternalInput").ap()
            for k, a in arrays.items()]
    out = nc.dram_tensor("out", (NODES, D), F32, kind="ExternalOutput").ap()
    gnn_kernel(nc, *args, out)
    r = run_bass_kernel_spmd(nc, [{f"in_{k}": a for k, a in arrays.items()}], core_ids=[0])
    return r.results[0]["out"]
```
